# Optimizing a Trainium2 kernel written in Bass

```python
import numpy as np
import jax
import jax.numpy as jnp

def _softmax(x, axis=-1):
    return jax.nn.softmax(x, axis=axis)

def _gelu(x):
    return jax.nn.gelu(x, approximate=True)

def _silu(x):
    return jax.nn.silu(x)

def _sigmoid(x):
    return jax.nn.sigmoid(x)

def _layernorm(x, axis=-1, eps=1e-05):
    m = jnp.mean(x, axis=axis, keepdims=True)
    v = jnp.var(x, axis=axis, keepdims=True)
    return (x - m) / jnp.sqrt(v + eps)

def _scatter_add(tgt, idx, src, axis=0):
    return tgt.at[idx].add(src)

def _segment_sum(src, seg, n):
    return jax.ops.segment_sum(src, seg, n)
kernel_name = 'mk_prb_d1_jaxref_r8_355042'

def setup_inputs(seed: int=0):
    np.random.seed(seed)
    _w = jnp.asarray

    def _L0_attn_setup():
        import jax, jax.numpy as jnp
        import numpy as np
        from jax import lax
        B, S, HID = (4, 256, 256)
        NH, DK, DV = (32, 64, 64)
        KDIM, VDIM = (NH * DK, NH * DV)
        CONV_DIM = 2 * KDIM + VDIM
        K_CONV = 4
        EPS = 1e-06

        def _l2norm(x):
            return x * lax.rsqrt(jnp.sum(x * x, -1, keepdims=True) + EPS)
        key = jax.random.key(seed)
        ks = jax.random.split(key, 8)
        return {'hidden_states': jax.random.normal(ks[0], (B, S, HID), jnp.float32), 'w_qkvz': jax.random.normal(ks[1], (2 * KDIM + 2 * VDIM, HID), jnp.float32) * 0.02, 'w_ba': jax.random.normal(ks[2], (2 * NH, HID), jnp.float32) * 0.02, 'conv_w': jax.random.normal(ks[3], (CONV_DIM, 1, K_CONV), jnp.float32) * 0.5, 'A_log': jnp.log(jax.random.uniform(ks[4], (NH,), jnp.float32, 0.1, 16.0)), 'dt_bias': jnp.ones((NH,), jnp.float32), 'norm_weight': jnp.ones((DV,), jnp.float32), 'w_out': jax.random.normal(ks[5], (HID, VDIM), jnp.float32) * 0.02}
    _L0_attn_in = _L0_attn_setup()

    def _L0_ffn_setup():
        import jax, jax.numpy as jnp
        import numpy as np
        HIDDEN = 256
        INTER = 1024
        SCALE = 64.0

        def fwht(x):
            orig_shape = x.shape
            n = orig_shape[-1]
            x = x.reshape(-1, n)
            h = 1
            while h < n:
                x = x.reshape(-1, n // (2 * h), 2, h)
                a, b = (x[:, :, 0, :], x[:, :, 1, :])
                x = jnp.stack([a + b, a - b], axis=2).reshape(-1, n)
                h *= 2
            return (x / jnp.sqrt(jnp.asarray(n, x.dtype))).reshape(orig_shape)
        key = jax.random.key(seed)
        ks = jax.random.split(key, 8)
        inp = jax.random.normal(ks[0], (4, 256, HIDDEN), dtype=jnp.float32)
        SU_ug = jnp.where(jax.random.bernoulli(ks[1], 0.5, (HIDDEN,)), 1.0, -1.0).astype(jnp.float32)
        SU_dp = jnp.where(jax.random.bernoulli(ks[2], 0.5, (INTER,)), 1.0, -1.0).astype(jnp.float32)
        Wscale_ug = jax.random.uniform(ks[3], (2 * INTER,), jnp.float32, 0.5, 1.5)
        Wscale_dp = jax.random.uniform(ks[4], (HIDDEN,), jnp.float32, 0.5, 1.5)
        W_up = jax.random.normal(ks[5], (INTER, HIDDEN), dtype=jnp.float32) * 0.02
        W_gate = jax.random.normal(ks[6], (INTER, HIDDEN), dtype=jnp.float32) * 0.02
        W_down = jax.random.normal(ks[7], (HIDDEN, INTER), dtype=jnp.float32) * 0.02
        return {'input': inp, 'SU_ug': SU_ug, 'SU_dp': SU_dp, 'Wscale_ug': Wscale_ug, 'Wscale_dp': Wscale_dp, 'W_up': W_up, 'W_gate': W_gate, 'W_down': W_down}
    _L0_ffn_in = _L0_ffn_setup()
    _d = {'L0_attn_hidden_states': _L0_attn_in['hidden_states'], 'L0_attn_w_qkvz': _L0_attn_in['w_qkvz'], 'L0_attn_w_ba': _L0_attn_in['w_ba'], 'L0_attn_conv_w': _L0_attn_in['conv_w'], 'L0_attn_A_log': _L0_attn_in['A_log'], 'L0_attn_dt_bias': _L0_attn_in['dt_bias'], 'L0_attn_norm_weight': _L0_attn_in['norm_weight'], 'L0_attn_w_out': _L0_attn_in['w_out'], 'L0_ffn_SU_ug': _L0_ffn_in['SU_ug'], 'L0_ffn_SU_dp': _L0_ffn_in['SU_dp'], 'L0_ffn_Wscale_ug': _L0_ffn_in['Wscale_ug'], 'L0_ffn_Wscale_dp': _L0_ffn_in['Wscale_dp'], 'L0_ffn_W_up': _L0_ffn_in['W_up'], 'L0_ffn_W_gate': _L0_ffn_in['W_gate'], 'L0_ffn_W_down': _L0_ffn_in['W_down']}
    _x0 = _d['L0_attn_hidden_states']
    _d['L0_attn_hidden_states'] = jax.random.normal(jax.random.fold_in(jax.random.key(seed), 1), (4, 256, 256), dtype=_x0.dtype)
    del _x0
    return _d

def reference(L0_attn_hidden_states, L0_attn_w_qkvz, L0_attn_w_ba, L0_attn_conv_w, L0_attn_A_log, L0_attn_dt_bias, L0_attn_norm_weight, L0_attn_w_out, L0_ffn_SU_ug, L0_ffn_SU_dp, L0_ffn_Wscale_ug, L0_ffn_Wscale_dp, L0_ffn_W_up, L0_ffn_W_gate, L0_ffn_W_down):

    def _L0_attn_ref(hidden_states, w_qkvz, w_ba, conv_w, A_log, dt_bias, norm_weight, w_out):
        import jax, jax.numpy as jnp
        import numpy as np
        from jax import lax
        B, S, HID = (4, 256, 256)
        NH, DK, DV = (32, 64, 64)
        KDIM, VDIM = (NH * DK, NH * DV)
        CONV_DIM = 2 * KDIM + VDIM
        K_CONV = 4
        EPS = 1e-06

        def _l2norm(x):
            return x * lax.rsqrt(jnp.sum(x * x, -1, keepdims=True) + EPS)
        Bsz, Sl, _ = hidden_states.shape
        qkvz = (hidden_states @ w_qkvz.T).reshape(Bsz, Sl, NH, 2 * DK + 2 * DV)
        q, k, v, z = jnp.split(qkvz, [DK, 2 * DK, 2 * DK + DV], axis=-1)
        ba = (hidden_states @ w_ba.T).reshape(Bsz, Sl, NH, 2)
        b, a = (ba[..., 0], ba[..., 1])
        mixed = jnp.concatenate([q.reshape(Bsz, Sl, -1), k.reshape(Bsz, Sl, -1), v.reshape(Bsz, Sl, -1)], -1)
        mixed = jnp.swapaxes(mixed, 1, 2)
        mixed = lax.conv_general_dilated(mixed, conv_w, (1,), [(K_CONV - 1, 0)], dimension_numbers=('NCH', 'OIH', 'NCH'), feature_group_count=CONV_DIM)
        mixed = jnp.swapaxes(mixed, 1, 2)
        qf, kf, vf = jnp.split(mixed, [KDIM, 2 * KDIM], axis=-1)
        q = qf.reshape(Bsz, Sl, NH, DK)
        k = kf.reshape(Bsz, Sl, NH, DK)
        v = vf.reshape(Bsz, Sl, NH, DV)
        g = -jnp.exp(A_log) * jax.nn.softplus(a + dt_bias)
        beta = jax.nn.sigmoid(b)
        q = _l2norm(q) * DK ** (-0.5)
        k = _l2norm(k)
        qs = jnp.moveaxis(q, 1, 0)
        ks_ = jnp.moveaxis(k, 1, 0)
        vs = jnp.moveaxis(v, 1, 0)
        gs = jnp.moveaxis(g, 1, 0)
        bs = jnp.moveaxis(beta, 1, 0)

        def step(Sstate, xs):
            q_t, k_t, v_t, g_t, b_t = xs
            Sstate = Sstate * jnp.exp(g_t)[..., None, None]
            kv = jnp.einsum('bhk,bhkv->bhv', k_t, Sstate)
            delta = (v_t - kv) * b_t[..., None]
            Sstate = Sstate + k_t[..., :, None] * delta[..., None, :]
            o_t = jnp.einsum('bhk,bhkv->bhv', q_t, Sstate)
            return (Sstate, o_t)
        S0 = jnp.zeros((Bsz, NH, DK, DV), q.dtype)
        _, o = lax.scan(step, S0, (qs, ks_, vs, gs, bs))
        o = jnp.moveaxis(o, 0, 1)
        var = jnp.mean(o * o, -1, keepdims=True)
        o = o * lax.rsqrt(var + EPS) * norm_weight * jax.nn.sigmoid(z)
        return o.reshape(Bsz, Sl, VDIM) @ w_out.T

    def _L0_ffn_ref(input, SU_ug, SU_dp, Wscale_ug, Wscale_dp, W_up, W_gate, W_down):
        import jax, jax.numpy as jnp
        import numpy as np
        HIDDEN = 256
        INTER = 1024
        SCALE = 64.0

        def fwht(x):
            orig_shape = x.shape
            n = orig_shape[-1]
            x = x.reshape(-1, n)
            h = 1
            while h < n:
                x = x.reshape(-1, n // (2 * h), 2, h)
                a, b = (x[:, :, 0, :], x[:, :, 1, :])
                x = jnp.stack([a + b, a - b], axis=2).reshape(-1, n)
                h *= 2
            return (x / jnp.sqrt(jnp.asarray(n, x.dtype))).reshape(orig_shape)
        n = SU_ug.shape[0]
        x = input.reshape(-1, n)
        x = fwht(x * SU_ug) / SCALE
        x_up = x @ W_up.T * (Wscale_ug[:INTER] * SCALE)
        x_gate = x @ W_gate.T * (Wscale_ug[INTER:] * SCALE)
        x = jax.nn.silu(x_gate) * x_up
        x = fwht(x * SU_dp) / SCALE
        x = x @ W_down.T * (Wscale_dp * SCALE)
        return x.reshape(input.shape)
    x = L0_attn_hidden_states
    xn = _layernorm(x, axis=-1)
    x = x + _L0_attn_ref(xn, L0_attn_w_qkvz, L0_attn_w_ba, L0_attn_conv_w, L0_attn_A_log, L0_attn_dt_bias, L0_attn_norm_weight, L0_attn_w_out) + _L0_ffn_ref(xn, L0_ffn_SU_ug, L0_ffn_SU_dp, L0_ffn_Wscale_ug, L0_ffn_Wscale_dp, L0_ffn_W_up, L0_ffn_W_gate, L0_ffn_W_down)
    return x

_drawn_inputs = setup_inputs


def setup_inputs(seed=0):
    import zlib

    import numpy as np

    out = dict(_drawn_inputs(seed))
    spreads = {'L0_attn_dt_bias': (1.0, 0.6), 'L0_attn_norm_weight': (1.0, 0.6)}
    factors = {'L0_ffn_Wscale_ug': 4.227,
     'L0_ffn_Wscale_dp': 5.881,
     'L0_attn_w_ba': 8.0,
     'L0_attn_A_log': 3.889}
    for name, (base, spread) in spreads.items():
        noise = np.random.default_rng([zlib.crc32(name.encode()), seed]).standard_normal(out[name].shape)
        drawn = base * np.exp(spread * noise) if base else spread * noise
        out[name] = jnp.asarray(drawn.astype(out[name].dtype))
    for name, factor in factors.items():
        out[name] = (out[name] * factor).astype(out[name].dtype)
    return out
```

```python
from contextlib import ExitStack

import numpy as np

import concourse.bass as bass
from concourse import mybir
from concourse.alu_op_type import AluOpType as ALU

F32 = mybir.dt.float32
BF16 = mybir.dt.bfloat16
ACT = mybir.ActivationFunctionType
AX = mybir.AxisListType

P = 128
B, S, HID = 4, 256, 256
NH, D = 32, 64
NTOK = B * S
KC = HID // P
PAIRS = NH // 2
C = 64
NCH = S // C
UNITS = B * NCH
TT = NTOK // P
INTER = 1024
IT = INTER // P
BLOCKS = [1, 2, 4, 8, 16, 32]
NL = len(BLOCKS) - 1
EPS = 1e-6
LN_EPS = 1e-5
GATE_FLOOR = -104.0

CONST = {}
_at = 0
for _name, _n in (("ident", P), ("eye", C), ("cum", C), ("strict_bd", P), ("cum_bd", P), ("swap", P),
                  ("neg", C), ("hsel", 2), ("level", C * len(BLOCKS)), ("had", P), ("half", UNITS), ("neghalf", UNITS)):
    CONST[_name] = (_at, _at + _n)
    _at += _n
NCONST = _at


def constants():
    c = np.zeros((P, NCONST), np.float32)

    def put(name, x):
        c[:, CONST[name][0]:CONST[name][1]] = x

    r, i = np.arange(P)[:, None], np.arange(C)[None, :]
    cc = np.arange(P)[None, :]
    j = r % C
    put("ident", r == cc)
    put("eye", j == i)
    put("cum", j <= i)
    put("strict_bd", (r // C == cc // C) & (r % C > cc % C))
    put("cum_bd", (r // C == cc // C) & (r % C <= cc % C))
    put("swap", r // C != cc // C)
    put("neg", np.where(j > i, -1e30, 0.0))
    put("hsel", r // C == np.arange(2)[None, :])
    put("level", np.concatenate([(j // (2 * s) == i // (2 * s)) & ((j // s) % 2 == 0) & ((i // s) % 2 == 1)
                                 for s in BLOCKS], axis=1))
    bits = np.array([[bin(a & b).count("1") % 2 for b in range(P)] for a in range(P)])
    put("had", 1.0 - 2.0 * bits)
    put("half", 0.5)
    put("neghalf", -0.5)
    return c


def build(nc, x, wqkvz, wba, conv, alog, dtb, nw, wout, su_ug, su_dp, ws_up, ws_gate, ws_dp,
          wup, wgate, wdown, consts, out):
    with ExitStack() as keep:
        def sb(name, shape, dt=F32, ctx=keep):
            return ctx.enter_context(nc.sbuf_tensor(name, [P] + shape, dt))

        def sem(name):
            return keep.enter_context(nc.semaphore(name))

        bank = [keep.enter_context(nc.psum_tensor(f"bank{i}", [P, 512], F32)) for i in range(8)]
        cst = sb("cst", [NCONST])

        def k(name):
            return cst[:, CONST[name][0]:CONST[name][1]]

        xnT = sb("xnT", [KC, NTOK])
        scal = sb("scal", [PAIRS, 4, UNITS])
        oT = sb("oT", [PAIRS, NTOK])
        negb = sb("negb", [C], BF16)
        identb = sb("identb", [P], BF16)
        yffn = sb("yffn", [TT, HID])

        setup_and_ffn(nc, sem, sb, bank, k, cst, xnT, scal, oT, negb, identb, yffn,
                      x, wba, alog, dtb, su_ug, su_dp, ws_up, ws_gate, ws_dp,
                      wup, wgate, wdown, consts)
        attention(nc, sem, sb, bank, k, xnT, scal, oT, negb, identb, wqkvz, conv)
        finish(nc, sem, sb, bank, oT, yffn, nw, wout, x, out)


def setup_and_ffn(nc, sem, sb, bank, k, cst, xnT, scal, oT, negb, identb, yffn,
                  x, wba, alog, dtb, su_ug, su_dp, ws_up, ws_gate, ws_dp,
                  wup, wgate, wdown, consts):
    with ExitStack() as ctx:
        def tmp(name, shape, dt=F32):
            return sb(name, shape, dt, ctx)

        xs = tmp("xs", [TT, HID])
        xc = tmp("xc", [TT, HID])
        xq = tmp("xq", [TT, HID])
        st = tmp("st", [4, TT])
        wbas = tmp("wbas", [KC, 2, 2 * PAIRS])
        ah = tmp("ah", [3, PAIRS])
        ga = tmp("ga", [8, PAIRS, UNITS])
        vec = tmp("vec", [KC + 3 * IT])
        wsd = tmp("wsd", [HID])
        wupT = tmp("wupT", [KC, INTER])
        wgaT = tmp("wgaT", [KC, INTER])
        wdT = tmp("wdT", [2, IT, HID])
        hug = tmp("hug", [KC, KC, P])
        xh = tmp("xh", [KC, NTOK])
        hT = oT[:, 0:IT, :]
        th = tmp("th", [2, 512])
        gl = tmp("gl", [2, 512])
        coef = tmp("coef", [2, IT])
        su, sd, wsu, wsg = (vec[:, a:a + n] for a, n in ((0, KC), (KC, IT), (KC + IT, IT), (KC + 2 * IT, IT)))

        x_in, const_in, gate_in, ffn_in = (sem(n) for n in ("x_in", "const_in", "gate_in", "ffn_in"))
        v_step, xt_ready, xt_used = sem("v_step"), sem("xt_ready"), sem("xt_used")
        ba_ready, a_step, cum_ready = sem("ba_ready"), sem("a_step"), sem("cum_ready")
        hug_made, xh_ready, xh_done = sem("hug_made"), sem("xh_ready"), sem("xh_done")
        wd_ready, wd_used, wd_done = sem("wd_ready"), sem("wd_used"), sem("wd_done")
        gu_ready, tanh_done, gu_used = sem("gu_ready"), sem("tanh_done"), sem("gu_used")
        y_ready, y_done = sem("y_ready"), sem("y_done")
        rstd_done = sem("rstd_done")
        steps = {}

        with nc.Block() as block:
            @block.sync
            def _(sp):
                sp.dma_start(xs[:], x.rearrange("(t p) d -> p t d", p=P)).then_inc(x_in, 16)
                sp.dma_start(cst[:], consts).then_inc(const_in, 16)
                sp.dma_start(wbas[:], wba).then_inc(gate_in, 16)
                for h in range(2):
                    rows = slice(h * C, h * C + C)
                    for m, src in enumerate((alog, dtb)):
                        sp.dma_start(ah[rows, m, :], src[1 - h:2 - h, :].broadcast_to([C, PAIRS])).then_inc(gate_in, 16)
                sp.dma_start(wdT[:, 0, :, :], wdown).then_inc(ffn_in, 16)
                for v, src in ((su, su_ug), (sd, su_dp), (wsu, ws_up), (wsg, ws_gate)):
                    sp.dma_start(v, src).then_inc(ffn_in, 16)
                sp.dma_start(wsd[:], ws_dp.broadcast_to([P, HID])).then_inc(ffn_in, 16)
                sp.dma_start(wupT[:], wup).then_inc(ffn_in, 16)
                sp.dma_start(wgaT[:], wgate).then_inc(ffn_in, 16)

            NFFN = 16 * 8

            @block.vector
            def _(dve):
                count = [0]

                def step(ins):
                    count[0] += 1
                    ins.then_inc(v_step, 1)
                    dve.wait_ge(v_step, count[0])

                def over(a, n):
                    return a.unsqueeze(2).broadcast_to([P, TT, n])

                dve.wait_ge(x_in, 16)
                step(nc.vector.tensor_reduce(st[:, 0, :], xs[:], AX.X, ALU.add))
                step(nc.vector.tensor_scalar(st[:, 1, :], st[:, 0, :], 1.0 / HID, None, ALU.mult))
                step(nc.vector.tensor_tensor(xc[:], xs[:], over(st[:, 1, :], HID), ALU.subtract))
                step(nc.vector.tensor_tensor(xq[:], xc[:], xc[:], ALU.mult))
                step(nc.vector.tensor_reduce(st[:, 2, :], xq[:], AX.X, ALU.add))
                step(nc.vector.tensor_scalar(st[:, 0, :], st[:, 2, :], 1.0 / HID, LN_EPS, ALU.mult, ALU.add))
                steps["var"] = count[0]
                dve.wait_ge(rstd_done, 1)
                step(nc.vector.tensor_tensor(xs[:], xc[:], over(st[:, 3, :], HID), ALU.mult))
                steps["xn"] = count[0]
                dve.wait_ge(const_in, 16)
                step(nc.vector.tensor_copy(negb[:], k("neg")))
                step(nc.vector.tensor_copy(identb[:], k("ident")))
                for q in range(1, 4, 2):
                    dve.wait_ge(xt_ready, q + 1)
                    nc.vector.tensor_copy(xnT[:, q // 2, (q % 2) * 512:(q % 2) * 512 + 512], bank[q][:]).then_inc(xt_used, 1)
                dve.wait_ge(ffn_in, NFFN)
                for kc in range(KC):
                    for mc in range(KC):
                        sign = (1.0 if not (kc and mc) else -1.0) / float(np.sqrt(HID))
                        nc.vector.tensor_scalar(hug[:, kc, mc, :], k("had"), su[:, kc:kc + 1], sign, ALU.mult, ALU.mult)\
                          .then_inc(hug_made, 1)
                step(nc.vector.tensor_tensor(coef[:, 0, :], wsg, wsu, ALU.mult))
                step(nc.vector.scalar_tensor_tensor(out=coef[:, 1, :], in0=coef[:, 0, :], scalar=0.5, in1=sd, op0=ALU.mult, op1=ALU.mult))
                step(nc.vector.tensor_scalar(coef[:, 0, :], wsg, 0.5, None, ALU.mult))
                steps["coef"] = count[0]
                dve.wait_ge(ba_ready, 1)
                step(nc.vector.tensor_copy(ga[:, 0:2, :, :].rearrange("p k h u -> p u k h"),
                                           bank[4][:].rearrange("p (u k h) -> p u k h", u=UNITS, k=2)))
                steps["ba"] = count[0]
                gb = lambda a: a.unsqueeze(2).broadcast_to([P, PAIRS, UNITS])
                step(nc.vector.tensor_tensor(ga[:, 2, :, :], ga[:, 1, :, :], gb(ah[:, 1, :]), ALU.add))
                step(nc.vector.scalar_tensor_tensor(out=ga[:, 3, :, :], in0=ga[:, 2, :, :], scalar=-1.0, in1=ga[:, 2, :, :],
                                                    op0=ALU.mult, op1=ALU.max))
                steps["abs"] = count[0]
                step(nc.vector.tensor_scalar(ga[:, 2, :, :], ga[:, 2, :, :], 0.0, None, ALU.max))
                dve.wait_ge(a_step, 2)
                step(nc.vector.tensor_scalar(ga[:, 0, :, :], ga[:, 4, :, :], 1.0, None, ALU.add))
                step(nc.vector.reciprocal(scal[:, :, 1, :], ga[:, 0, :, :]))
                dve.wait_ge(a_step, 3)
                step(nc.vector.tensor_scalar(ga[:, 0, :, :], ga[:, 5, :, :], 2.0, None, ALU.add))
                step(nc.vector.reciprocal(ga[:, 6, :, :], ga[:, 0, :, :]))
                step(nc.vector.tensor_tensor(ga[:, 0, :, :], ga[:, 5, :, :], ga[:, 6, :, :], ALU.mult))
                step(nc.vector.tensor_tensor(ga[:, 1, :, :], ga[:, 0, :, :], ga[:, 0, :, :], ALU.mult))
                step(nc.vector.tensor_scalar(ga[:, 6, :, :], ga[:, 1, :, :], 1.0 / 17, 1.0 / 15, ALU.mult, ALU.add))
                for m in (13, 11, 9, 7, 5, 3, 1):
                    step(nc.vector.tensor_tensor(ga[:, 6, :, :], ga[:, 6, :, :], ga[:, 1, :, :], ALU.mult))
                    step(nc.vector.tensor_scalar(ga[:, 6, :, :], ga[:, 6, :, :], 1.0 / m, None, ALU.add))
                step(nc.vector.tensor_tensor(ga[:, 6, :, :], ga[:, 6, :, :], ga[:, 0, :, :], ALU.mult))
                step(nc.vector.scalar_tensor_tensor(out=ga[:, 6, :, :], in0=ga[:, 6, :, :], scalar=2.0, in1=ga[:, 2, :, :],
                                                    op0=ALU.mult, op1=ALU.add))
                step(nc.vector.tensor_scalar(ah[:, 2, :], ah[:, 0, :], -1.0, None, ALU.mult))
                step(nc.vector.tensor_tensor(ga[:, 7, :, :], ga[:, 6, :, :], gb(ah[:, 2, :]), ALU.mult))
                step(nc.vector.tensor_scalar(scal[:, :, 0, :], ga[:, 7, :, :], GATE_FLOOR, None, ALU.max))
                step(nc.vector.tensor_scalar(ga[:, 7, :, :], ga[:, 7, :, :], GATE_FLOOR, None, ALU.max))
                steps["g"] = count[0]
                dve.wait_ge(wd_used, 4)
                for h in (1, 2, 4):
                    src, dst = (wdT[:, 1], wdT[:, 0]) if h != 2 else (wdT[:, 0], wdT[:, 1])
                    s4 = src.rearrange("p (a t h) d -> p a t (h d)", t=2, h=h)
                    d4 = dst.rearrange("p (a t h) d -> p a t (h d)", t=2, h=h)
                    nc.vector.tensor_tensor(d4[:, :, 0], s4[:, :, 0], s4[:, :, 1], ALU.add)
                    step(nc.vector.tensor_tensor(d4[:, :, 1], s4[:, :, 0], s4[:, :, 1], ALU.subtract))
                nc.vector.scalar_tensor_tensor(
                    out=wdT[:, 1], in0=wdT[:, 0], scalar=1.0 / float(np.sqrt(INTER)),
                    in1=wsd[:].unsqueeze(1).broadcast_to([P, IT, HID]), op0=ALU.mult, op1=ALU.mult).then_inc(wd_done, 1)
                for n in range(2 * IT):
                    i, t = n // 2, n % 2
                    dve.wait_ge(tanh_done, n + 1)
                    g, u = bank[2 * (n % 2)], bank[2 * (n % 2) + 1]
                    step(nc.vector.scalar_tensor_tensor(out=gl[:, n % 2, :], in0=th[:, n % 2, :], scalar=1.0, in1=g[:],
                                                        op0=ALU.add, op1=ALU.mult))
                    nc.vector.scalar_tensor_tensor(out=hT[:, i, t * 512:t * 512 + 512], in0=u[:], scalar=coef[:, 1, i:i + 1],
                                                   in1=gl[:, n % 2, :], op0=ALU.mult, op1=ALU.mult).then_inc(gu_used, 1)
                for t in range(0, TT, 2):
                    dve.wait_ge(y_ready, t // 2 + 1)
                    nc.vector.tensor_copy(yffn[:, t:t + 2, :], bank[4 + (t // 2) % 2][:].rearrange("p (t d) -> p t d", t=2))\
                      .then_inc(y_done, 1)

            @block.gpsimd
            def _(pool):
                pool.wait_ge(const_in, 16)
                pool.wait_ge(v_step, steps["var"])
                nc.gpsimd.tensor_tensor(st[:, 3, :], st[:, 0, :], k("neghalf")[:, 0:TT], ALU.pow).then_inc(rstd_done, 1)

            @block.scalar
            def _(act):
                for q in range(0, 4, 2):
                    act.wait_ge(xt_ready, q + 1)
                    nc.scalar.activation(xnT[:, q // 2, 0:512], bank[q][:], ACT.Copy).then_inc(xt_used, 1)
                act.wait_ge(gate_in, 16 * 5)
                nc.scalar.activation(ah[:, 0, :], ah[:, 0, :], ACT.Exp).then_inc(a_step, 1)
                act.wait_ge(v_step, steps["ba"])
                nc.scalar.activation(ga[:, 4, :, :], ga[:, 0, :, :], ACT.Exp, scale=-1.0).then_inc(a_step, 1)
                act.wait_ge(v_step, steps["abs"])
                nc.scalar.activation(ga[:, 5, :, :], ga[:, 3, :, :], ACT.Exp, scale=-1.0).then_inc(a_step, 1)
                for m in range(KC * 2):
                    act.wait_ge(xh_ready, m + 1)
                    nc.scalar.activation(xh[:, m // 2, (m % 2) * 512:(m % 2) * 512 + 512], bank[m][:], ACT.Copy).then_inc(xh_done, 1)
                for m in range(4):
                    act.wait_ge(wd_ready, m + 1)
                    nc.scalar.activation(wdT[:, 1, 2 * m:2 * m + 2, :], bank[4 + m][:].rearrange("p (t d) -> p t d", t=2), ACT.Copy)\
                      .then_inc(wd_used, 1)
                act.wait_ge(cum_ready, 1)
                for m in range(2):
                    nc.scalar.activation(scal[:, :, 2 + m, :], bank[5][:, m * 256:m * 256 + 256].rearrange("p (h u) -> p h u", h=PAIRS),
                                         ACT.Exp).then_inc(a_step, 1)
                act.wait_ge(v_step, steps["coef"])
                for n in range(2 * IT):
                    act.wait_ge(gu_ready, n + 1)
                    if n >= 2:
                        act.wait_ge(gu_used, n - 1)
                    nc.scalar.activation(th[:, n % 2, :], bank[2 * (n % 2)][:], ACT.Tanh, scale=coef[:, 0, n // 2:n // 2 + 1]).then_inc(tanh_done, 1)

            @block.tensor
            def _(pe):
                pe.wait_ge(const_in, 16)
                pe.wait_ge(v_step, steps["xn"])
                for q in range(4):
                    kc, t0 = q // 2, 4 * (q % 2)
                    for t in range(4):
                        last = nc.tensor.transpose(bank[q][:, t * P:t * P + P], xs[:, t0 + t, kc * P:kc * P + P], k("ident"))
                    last.then_inc(xt_ready, 1)
                pe.wait_ge(xt_used, 4)
                pe.wait_ge(gate_in, 16 * 5)
                for u in range(UNITS):
                    for h in range(2):
                        for kc in range(KC):
                            last = nc.tensor.matmul(bank[4][h * C:h * C + C, u * 2 * PAIRS:(u + 1) * 2 * PAIRS],
                                                    xnT[:, kc, u * C:u * C + C], wbas[:, kc, h, :], start=kc == 0, stop=kc == KC - 1)
                last.then_inc(ba_ready, 1)
                pe.wait_ge(hug_made, 4)
                for m in range(KC * 2):
                    for kc in range(KC):
                        last = nc.tensor.matmul(bank[m][:], hug[:, kc, m // 2, :], xnT[:, kc, (m % 2) * 512:(m % 2) * 512 + 512],
                                                start=kc == 0, stop=kc == KC - 1)
                    last.then_inc(xh_ready, 1)
                pe.wait_ge(v_step, steps["ba"])
                pe.wait_ge(ffn_in, NFFN)
                for m in range(4):
                    nc.tensor.matmul(bank[4 + m][:], k("had"), wdT[:, 0, 2 * m:2 * m + 2, :], start=True, stop=True).then_inc(wd_ready, 1)
                pe.wait_ge(wd_used, 4)
                pe.wait_ge(v_step, steps["g"])
                nc.tensor.matmul(bank[5][:, 0:256], k("cum_bd"), ga[:, 7, :, :], start=True, stop=True)
                nc.tensor.matmul(bank[5][:, 256:512], k("strict_bd"), ga[:, 7, :, :], start=True, stop=True).then_inc(cum_ready, 1)
                pe.wait_ge(xh_done, 4)
                for n in range(2 * IT):
                    i, t = n // 2, n % 2
                    if n >= 2:
                        pe.wait_ge(gu_used, n - 1)
                    for w, dst in ((wgaT, bank[2 * (n % 2)]), (wupT, bank[2 * (n % 2) + 1])):
                        for kc in range(KC):
                            last = nc.tensor.matmul(dst[:], w[:, kc, i * P:i * P + P], xh[:, kc, t * 512:t * 512 + 512],
                                                    start=kc == 0, stop=kc == KC - 1)
                    last.then_inc(gu_ready, 1)
                pe.wait_ge(gu_used, 2 * IT)
                pe.wait_ge(wd_done, 1)
                pe.wait_ge(a_step, 5)
                for t in range(TT):
                    if t % 2 == 0 and t >= 4:
                        pe.wait_ge(y_done, t // 2 - 1)
                    for i in range(IT):
                        last = nc.tensor.matmul(bank[4 + (t // 2) % 2][:, (t % 2) * HID:(t % 2) * HID + HID],
                                                hT[:, i, t * P:t * P + P], wdT[:, 1, i, :], start=i == 0, stop=i == IT - 1)
                    if t % 2:
                        last.then_inc(y_ready, 1)


def attention(nc, sem, sb, bank, k, xnT, scal, oT, negb, identb, wqkvz, conv):
    with ExitStack() as ctx:
        def tmp(name, shape, dt=F32):
            return sb(name, shape, dt, ctx)

        W4 = NCH * C
        wq = tmp("wq", [KC, 4, P])
        cw = tmp("cw", [3, 4])
        sc = tmp("sc", [4, UNITS])
        kq = tmp("kq", [3, NTOK])
        zt = tmp("zt", [TT, P])
        gm = tmp("gm", [B, NCH, C])
        gg = tmp("gg", [B, 2, NCH, C])
        gb_ = tmp("gb", [2, NCH, C])
        dtmp = tmp("dtmp", [NCH, C])
        stat = tmp("stat", [6, UNITS])
        AT = tmp("AT", [2, NCH, C])
        ME = tmp("ME", [B, len(BLOCKS), NCH, C])
        UT = tmp("UT", [B, 2, NCH, C])
        sqq = UT[:, 0:2].rearrange("p b k u c -> p (b k u c)")
        ET = tmp("ET", [2, NCH, C])
        LA = tmp("LA", [2, UNITS, C])
        LBo = tmp("LBo", [2, UNITS, C])
        LBs = tmp("LBs", [2, UNITS, C])
        R = tmp("R", [2, UNITS, C])
        kc_ = tmp("kc", [2, NCH, C])
        kg = tmp("kg", [B, NCH, C])
        qs = tmp("qs", [TT, 2])
        sqo = tmp("sqo", [B * 2, D])
        ost = tmp("ost", [3, B * 2])
        on = tmp("on", [B * 2, D])
        og = tmp("og", [B, P])

        names = ("loaded proj_done tap0_done conv_step z_done gm_done dg_done gexp_done gram_done scale_step gb_done "
                 "at_done pt_done mask_done trk_done kc_done trv_done v_done kg_done lb_done sqq_done qst_done qs_done "
                 "u1_done t1_ready t1_done et_ready et_done dn_ready ut_done w_ready w_done dl_ready dl_done "
                 "st_ready st_done o_ready osq_done ost_step og_done ogT_ready pair_done").split()
        s = {n: sem(n) for n in names}
        (loaded, proj_done, tap0_done, conv_step, z_done, gm_done, dg_done, gexp_done, gram_done, scale_step, gb_done,
         at_done, pt_done, mask_done, trk_done, kc_done, trv_done, v_done, kg_done, lb_done, sqq_done, qst_done, qs_done,
         u1_done, t1_ready, t1_done, et_ready, et_done, dn_ready, ut_done, w_ready, w_done, dl_ready, dl_done,
         st_ready, st_done, o_ready, osq_done, ost_step, og_done, ogT_ready, pair_done) = (s[n] for n in names)
        s0_zero, root_done, rms_done = sem("s0_zero"), sem("root_done"), sem("rms_done")

        turn = sem("turn")
        ring = [bank[0], bank[1]]
        DG, GR, TR = bank[2], bank[3], bank[4]
        IA, IB = [bank[5], bank[7]], [bank[6], bank[0]]
        OB = bank[7]
        tok, dk = (slice(C, P), slice(0, C)), (slice(0, C), slice(C, P))
        NJ = NL * B
        NUT = (NL - 1) * B + 2 * B

        def w4(ap):
            return ap.rearrange("p (u c) -> p u c", u=NCH)

        def over(a):
            return a.unsqueeze(2).broadcast_to([a.shape[0], a.shape[1], C])

        def each(a, n=NCH):
            return a.unsqueeze(1).broadcast_to([a.shape[0], n, C])

        with nc.Block() as block:
            @block.sync
            def _(sp):
                with sp.Fori(0, PAIRS) as n:
                    sp.wait_ge(pair_done, n * 2)
                    sp.dma_start(wq[:], wqkvz[bass.ds(n, 1)].rearrange("o p c t m -> (o p) c t m")).then_inc(loaded, 16)
                    sp.dma_start(cw[:], conv[bass.ds(n, 1)].rearrange("o p t m -> (o p) t m")).then_inc(loaded, 16)
                    sp.dma_start(sc[:], scal[:, bass.ds(n, 1)].rearrange("p o k u -> p (o k) u")).then_inc(loaded, 16)

            @block.tensor
            def _(pe):
                def alone():
                    pe.sem_inc(turn, 1)

                with pe.Fori(0, PAIRS) as n:
                    pe.wait_ge(loaded, n * 48 + 48)
                    pe.wait_ge(pair_done, n * 2)
                    for i in range(8):
                        if i >= 2:
                            pe.wait_ge(conv_step, n * 18 + 3 * (i - 1))
                        dst = ring[i % 2]
                        if i < 6:
                            for kc in range(KC):
                                last = nc.tensor.matmul(dst[:], wq[:, kc, i % 3, :], xnT[:, kc, (i // 3) * 512:(i // 3) * 512 + 512],
                                                        start=kc == 0, stop=kc == KC - 1)
                        else:
                            for t in range(4):
                                for kc in range(KC):
                                    tt = 4 * (i - 6) + t
                                    last = nc.tensor.matmul(dst[:, t * P:t * P + P], xnT[:, kc, tt * P:tt * P + P], wq[:, kc, 3, :],
                                                            start=kc == 0, stop=kc == KC - 1)
                        last.then_inc(proj_done, 1)
                    for b in range(B):
                        pe.wait_ge(gm_done, n * B + b + 1)
                        pe.wait_ge(gexp_done, n * B + b)
                        nc.tensor.matmul(DG[:, 0:W4], k("strict_bd"), gm[:, b], start=True, stop=False)
                        nc.tensor.matmul(DG[:, 0:W4], identb[:], each(negb[:]), start=False, stop=True)
                        nc.tensor.matmul(DG[:, W4:2 * W4], k("swap"), gm[:, b], start=True, stop=True).then_inc(dg_done, 1)
                        pe.wait_ge(conv_step, n * 18 + 3 * (3 * (b // 2) + 3))
                        pe.wait_ge(v_done, n * 2 * B + 2 * b)
                        alone()
                        for u in range(NCH):
                            t0 = b * S + u * C
                            for h in range(2):
                                last = nc.tensor.matmul(TR[tok[h], u * C:u * C + C], kq[dk[h], 0, t0:t0 + C], k("eye")[dk[h]], start=True, stop=True)
                        last.then_inc(trk_done, 1)
                        pe.wait_ge(pt_done, n * 2 * B + 2 * b)
                        alone()
                        for u in range(NCH):
                            t0 = b * S + u * C
                            for h in range(2):
                                last = nc.tensor.matmul(GR[tok[h], u * P:u * P + P], kq[dk[h], 0, t0:t0 + C], kq[dk[h], 0:2, t0:t0 + C],
                                                        start=True, stop=True)
                        last.then_inc(gram_done, 1)
                        pe.wait_ge(kc_done, n * B + b + 1)
                        alone()
                        for u in range(NCH):
                            t0 = b * S + u * C
                            for h in range(2):
                                last = nc.tensor.matmul(TR[tok[h], u * C:u * C + C], kq[dk[h], 2, t0:t0 + C], k("eye")[dk[h]], start=True, stop=True)
                        last.then_inc(trv_done, 1)
                    pe.wait_ge(sqq_done, n + 1)
                    pe.wait_ge(v_done, (n + 1) * 2 * B)
                    for t in range(TT):
                        last = nc.tensor.matmul(TR[:, 2 * t:2 * t + 2], sqq[:, t * P:t * P + P], k("hsel"), start=True, stop=True)
                    last.then_inc(qst_done, 1)
                    pe.wait_ge(z_done, n * 2 + 2)
                    for b in range(B):
                        pe.wait_ge(u1_done, n * B + b + 1)
                        if b >= 2:
                            pe.wait_ge(t1_done, n * B + b - 1)
                        alone()
                        for u in range(NCH):
                            for h in range(2):
                                last = nc.tensor.matmul(IB[b % 2][tok[1 - h], u * C:u * C + C], UT[tok[1 - h], b, 0, u, :],
                                                        k("eye")[tok[1 - h]], start=True, stop=True)
                        last.then_inc(t1_ready, 1)
                    pe.wait_ge(t1_done, n * B + B)

                    def merge_first(j):
                        l, b = j // B, j % B
                        if l > 0:
                            pe.wait_ge(ut_done, n * NUT + j - B + 1)
                        pe.wait_ge(mask_done, n * B * len(BLOCKS) + b * len(BLOCKS) + l + 2)
                        if j >= 2:
                            pe.wait_ge(et_done, n * NJ + j - 1)
                        alone()
                        for u in range(NCH):
                            for h in range(2):
                                last = nc.tensor.matmul(IA[j % 2][tok[h], u * C:u * C + C], ME[tok[h], b, l + 1, u, :],
                                                        UT[tok[h], b, 1, u, :], start=True, stop=True)
                        last.then_inc(et_ready, 1)

                    def merge_second(j):
                        l, b = j // B, j % B
                        pe.wait_ge(et_done, n * NJ + j + 1)
                        if j >= 2:
                            jj = j - 2
                            pe.wait_ge(ut_done, n * NUT + jj + 1 + max(0, jj + 1 - (NL - 1) * B))
                        alone()
                        for u in range(NCH):
                            for h in range(2):
                                last = nc.tensor.matmul(IB[j % 2][tok[h], u * C:u * C + C], ET[tok[h], j % 2, u, :],
                                                        UT[tok[h], b, 0, u, :], start=True, stop=True)
                                if l < NL - 1:
                                    last = nc.tensor.matmul(IB[j % 2][tok[h], W4 + u * C:W4 + u * C + C], UT[tok[h], b, 0, u, :],
                                                            ET[tok[h], j % 2, u, :], start=True, stop=True)
                        last.then_inc(dn_ready, 1)

                    merge_first(0)
                    for j in range(NJ):
                        if j + 1 < NJ:
                            merge_first(j + 1)
                        merge_second(j)
                    for b in range(B):
                        pe.wait_ge(ut_done, n * NUT + (NL - 1) * B + 2 * b + 2)
                        pe.wait_ge(kg_done, n * B + b + 1)
                        if b == 0:
                            pe.wait_ge(et_done, n * NJ + NJ)
                        if b >= 2:
                            pe.wait_ge(w_done, n * 2 * B + 2 * (b - 1))
                        alone()
                        for u in range(NCH):
                            for h in range(2):
                                last = nc.tensor.matmul(IA[b % 2][dk[h], u * C:u * C + C], kg[tok[h], b, u, :],
                                                        LA[tok[h], h, b * NCH + u, :], start=True, stop=True)
                        last.then_inc(w_ready, 1)
                    pe.wait_ge(w_done, n * 2 * B + 2 * B)
                    pe.wait_ge(lb_done, n * 6 * B + 6 * B)
                    pe.wait_ge(qs_done, n + 1)
                    for c in range(NCH):
                        if c >= 1:
                            pe.wait_ge(st_done, n * 2 * (NCH - 1) + 2 * c)
                        for b in range(B):
                            for h in range(2):
                                u = b * NCH + c
                                last = nc.tensor.matmul(IA[0][tok[h], b * C:b * C + C], LA[:, h, u, :], R[:, h, u, :], start=True, stop=True)
                        last.then_inc(dl_ready, 1)
                        pe.wait_ge(dl_done, n * 2 * NCH + 2 * c + 2)
                        if c < NCH - 1:
                            for b in range(B):
                                for h in range(2):
                                    u = b * NCH + c
                                    last = nc.tensor.matmul(IB[0][dk[h], b * C:b * C + C], LBs[:, h, u, :], R[:, h, u, :], start=True, stop=True)
                            last.then_inc(st_ready, 1)
                        if c == 2:
                            pe.wait_ge(ost_step, n * 8 + 3)
                        for b in range(B):
                            for h in range(2):
                                u = b * NCH + c
                                r = (c % 2) * C
                                last = nc.tensor.matmul(OB[r:r + C, b * P + h * C:b * P + h * C + C], LBo[:, h, u, :], R[:, h, u, :],
                                                        start=True, stop=True)
                        last.then_inc(o_ready, 1)
                        if c % 2:
                            t = c // 2
                            pe.wait_ge(og_done, n * 2 + t + 1)
                            if t:
                                pe.wait_ge(pair_done, n * 2 + 1)
                            for b in range(B):
                                last = nc.tensor.transpose(TR[:, b * P:b * P + P], og[:, b, :], k("ident"))
                            last.then_inc(ogT_ready, 1)

            @block.scalar
            def _(act):
                with act.Fori(0, PAIRS) as n:
                    act.wait_ge(loaded, n * 48 + 48)
                    for i in range(6):
                        act.wait_ge(proj_done, n * 8 + i + 1)
                        nc.scalar.activation(kq[:, i % 3, (i // 3) * 512:(i // 3) * 512 + 512], ring[i % 2][:], ACT.Copy,
                                             scale=cw[:, i % 3, 3:4]).then_inc(tap0_done, 1)
                    for i in range(2):
                        act.wait_ge(proj_done, n * 8 + 7 + i)
                        nc.scalar.activation(zt[:, 4 * i:4 * i + 4, :], ring[i][:].rearrange("p (t m) -> p t m", t=4), ACT.Tanh,
                                             scale=0.5).then_inc(z_done, 1)
                    for b in range(B):
                        act.wait_ge(dg_done, n * B + b + 1)
                        nc.scalar.activation(gg[:, b], DG[:].rearrange("p (k u c) -> p k u c", k=2, u=NCH), ACT.Exp).then_inc(gexp_done, 1)
                        act.wait_ge(trk_done, n * B + b + 1)
                        if b >= 2:
                            act.wait_ge(lb_done, n * 6 * B + 6 * (b - 1))
                        nc.scalar.activation(kc_[:, b % 2], w4(TR[:, 0:W4]), ACT.Copy).then_inc(kc_done, 1)
                    act.wait_ge(conv_step, n * 18 + 18)
                    nc.scalar.activation(sqq, kq[:, 1, :], ACT.Square).then_inc(sqq_done, 1)
                    for b in range(B):
                        act.wait_ge(t1_ready, n * B + b + 1)
                        nc.scalar.activation(UT[:, b, 1], w4(IB[b % 2][:, 0:W4]), ACT.Copy).then_inc(t1_done, 1)
                    for j in range(NJ):
                        act.wait_ge(et_ready, n * NJ + j + 1)
                        if j >= 2:
                            act.wait_ge(dn_ready, n * NJ + j - 1)
                        nc.scalar.activation(ET[:, j % 2], w4(IA[j % 2][:, 0:W4]), ACT.Copy).then_inc(et_done, 1)
                    for b in range(B):
                        act.wait_ge(w_ready, n * B + b + 1)
                        for h in range(2):
                            nc.scalar.activation(LA[dk[h], h, b * NCH:(b + 1) * NCH, :], w4(IA[b % 2][dk[h], 0:W4]), ACT.Copy,
                                                 scale=-1.0).then_inc(w_done, 1)
                    Ru = R[:].rearrange("p h (b c) d -> p h b c d", b=B)
                    for c in range(NCH):
                        act.wait_ge(dl_ready, n * NCH + c + 1)
                        nc.scalar.activation(Ru[tok[0], 0, :, c, :], w4(IA[0][tok[0], 0:W4]), ACT.Copy).then_inc(dl_done, 1)
                        if c < NCH - 1:
                            act.wait_ge(st_ready, n * (NCH - 1) + c + 1)
                            nc.scalar.activation(Ru[dk[0], 0, :, c + 1, :], w4(IB[0][dk[0], 0:W4]), ACT.Copy).then_inc(st_done, 1)
                        if c % 2:
                            t = c // 2
                            act.wait_ge(o_ready, n * NCH + c + 1)
                            if t:
                                act.wait_ge(ost_step, n * 8 + 1)
                            nc.scalar.activation(sqo[:], OB[:].rearrange("p (b d) -> p b d", d=D), ACT.Square).then_inc(osq_done, 1)
                            act.wait_ge(ogT_ready, n * 2 + t + 1)
                            dst = oT[:, bass.ds(n, 1), :].rearrange("p o (b t m) -> p (o b) t m", b=B, t=2)[:, :, t, :]
                            nc.scalar.activation(dst, TR[:].rearrange("p (b m) -> p b m", b=B), ACT.Copy).then_inc(pair_done, 1)

            @block.gpsimd
            def _(pool):
                nc.gpsimd.memset(R[:], 0.0).then_inc(s0_zero, 1)
                with pool.Fori(0, PAIRS) as n:
                    pool.wait_ge(loaded, n * 48 + 48)
                    pool.wait_ge(pair_done, n * 2)
                    for b in range(B):
                        nc.gpsimd.tensor_tensor(gm[:, b], over(sc[:, 0, b * NCH:(b + 1) * NCH]), each(k("cum")), ALU.mult).then_inc(gm_done, 1)
                    for b in range(B):
                        us = slice(b * NCH, (b + 1) * NCH)
                        pool.wait_ge(gexp_done, n * B + b + 1)
                        pool.wait_ge(scale_step, n * 6 * B + 6 * b + 3)
                        nc.gpsimd.tensor_tensor(stat[:, 2, us], stat[:, 5, us], k("half")[:, 0:NCH], ALU.pow).then_inc(root_done, 1)
                        pool.wait_ge(scale_step, n * 6 * B + 6 * b + 5)
                        if b >= 2:
                            pool.wait_ge(pt_done, n * 2 * B + 2 * (b - 1))
                        nc.gpsimd.tensor_tensor(gb_[:, b % 2], gg[:, b, 0], over(stat[:, 3, us]), ALU.mult).then_inc(gb_done, 1)
                        pool.wait_ge(kc_done, n * B + b + 1)
                        nc.gpsimd.tensor_tensor(kg[:, b], kc_[:, b % 2], over(sc[:, 2, us]), ALU.mult).then_inc(kg_done, 1)
                        pool.wait_ge(at_done, n * B + b + 1)
                        for l in range(len(BLOCKS)):
                            nc.gpsimd.tensor_tensor(ME[:, b, l], AT[:, b % 2], each(k("level")[:, l * C:(l + 1) * C]), ALU.mult).then_inc(mask_done, 1)
                        pool.wait_ge(scale_step, n * 6 * B + 6 * b + 6)
                        pool.wait_ge(conv_step, n * 18 + 3 * (3 * (b // 2) + 2))
                        base = n * 6 * B + 6 * b
                        for half in range(2):
                            hq, hk = (0, 1) if half == 0 else (1, 0)
                            if half:
                                pool.wait_ge(lb_done, base + 3)
                            qT = kq[dk[hq], 1, b * S:(b + 1) * S].rearrange("p (u c) -> p u c", u=NCH)
                            nc.gpsimd.tensor_tensor(LBo[dk[hq], hq, us, :], qT, gg[dk[hq], b, 1], ALU.mult).then_inc(lb_done, 1)
                            nc.gpsimd.tensor_tensor(LBs[dk[hq], hq, us, :], each(k("eye")[dk[hq]]),
                                                    gg[dk[hq], b, 1, :, C - 1:C].broadcast_to([C, NCH, C]), ALU.mult).then_inc(lb_done, 1)
                            nc.gpsimd.tensor_tensor(LBs[tok[hk], hk, us, :], kc_[tok[hk], b % 2], over(stat[tok[hk], 4, us]), ALU.mult).then_inc(lb_done, 1)
                        pool.wait_ge(lb_done, base + 6)
                    for t in range(2):
                        pool.wait_ge(ost_step, n * 8 + 4 * t + 2)
                        nc.gpsimd.tensor_tensor(ost[:, 2, :], ost[:, 1, :], k("neghalf")[:, 0:B * 2], ALU.pow).then_inc(rms_done, 1)

            @block.vector
            def _(dve):
                dve.wait_ge(s0_zero, 1)
                with dve.Fori(0, PAIRS) as n:
                    for i in range(6):
                        y = kq[:, i % 3, (i // 3) * 512:(i // 3) * 512 + 512].rearrange("p (b s) -> p b s", b=2)
                        p = ring[i % 2][:].rearrange("p (b s) -> p b s", b=2)
                        dve.wait_ge(tap0_done, n * 6 + i + 1)
                        for m in (1, 2, 3):
                            nc.vector.scalar_tensor_tensor(out=y[:, :, m:S], in0=p[:, :, 0:S - m], scalar=cw[:, i % 3, 3 - m:4 - m],
                                                           in1=y[:, :, m:S], op0=ALU.mult, op1=ALU.add).then_inc(conv_step, 1)
                            dve.wait_ge(conv_step, n * 18 + 3 * i + m)
                    for b in range(B):
                        us = slice(b * NCH, (b + 1) * NCH)
                        base = n * 6 * B + 6 * b
                        gr = GR[:].rearrange("p (u k c) -> p u k c", u=NCH, k=2)
                        dve.wait_ge(gram_done, n * B + b + 1)
                        nc.vector.tensor_tensor(dtmp[:], gr[:, :, 0, :], each(k("eye")), ALU.mult).then_inc(scale_step, 1)
                        dve.wait_ge(scale_step, base + 1)
                        nc.vector.tensor_reduce(stat[:, 0, us], dtmp[:], AX.X, ALU.add).then_inc(scale_step, 1)
                        dve.wait_ge(scale_step, base + 2)
                        nc.vector.tensor_scalar(stat[:, 5, us], stat[:, 0, us], EPS, None, ALU.add).then_inc(scale_step, 1)
                        dve.wait_ge(scale_step, base + 3)
                        nc.vector.reciprocal(stat[:, 1, us], stat[:, 5, us]).then_inc(scale_step, 1)
                        dve.wait_ge(scale_step, base + 4)
                        nc.vector.tensor_tensor(stat[:, 3, us], stat[:, 1, us], sc[:, 1, us], ALU.mult).then_inc(scale_step, 1)
                        dve.wait_ge(scale_step, base + 5)
                        nc.vector.tensor_tensor(stat[:, 4, us], stat[:, 3, us], sc[:, 3, us], ALU.mult).then_inc(scale_step, 1)
                        dve.wait_ge(gb_done, n * B + b + 1)
                        if b >= 2:
                            dve.wait_ge(mask_done, (n * B + b - 1) * len(BLOCKS))
                        nc.vector.tensor_tensor(AT[:, b % 2], gr[:, :, 0, :], gb_[:, b % 2], ALU.mult).then_inc(at_done, 1)
                        for h in range(2):
                            nc.vector.tensor_tensor(LBo[tok[h], h, us, :], gr[tok[h], :, 1, :], gb_[tok[h], b % 2], ALU.mult).then_inc(pt_done, 1)
                        dve.wait_ge(trv_done, n * B + b + 1)
                        dve.wait_ge(root_done, n * B + b + 1)
                        for h in range(2):
                            nc.vector.tensor_tensor(R[tok[h], h, us, :], w4(TR[tok[h], 0:W4]), over(stat[tok[h], 2, us]), ALU.mult).then_inc(v_done, 1)
                    dve.wait_ge(qst_done, n + 1)
                    nc.vector.tensor_scalar(qs[:], TR[:, 0:2 * TT].rearrange("p (t h) -> p t h", h=2), EPS, EPS * D, ALU.add, ALU.mult).then_inc(qs_done, 1)
                    for b in range(B):
                        dve.wait_ge(mask_done, n * B * len(BLOCKS) + b * len(BLOCKS) + 1)
                        nc.vector.tensor_tensor(UT[:, b, 0], each(k("eye")), ME[:, b, 0], ALU.subtract).then_inc(u1_done, 1)
                    for j in range(NJ):
                        l, b = j // B, j % B
                        dve.wait_ge(dn_ready, n * NJ + j + 1)
                        src = IB[j % 2]
                        if l < NL - 1:
                            nc.vector.tensor_tensor(UT[:, b], UT[:, b], src[:].rearrange("p (k u c) -> p k u c", k=2, u=NCH), ALU.subtract)\
                              .then_inc(ut_done, 1)
                        else:
                            for h in range(2):
                                nc.vector.tensor_tensor(LA[tok[h], h, b * NCH:(b + 1) * NCH, :], UT[tok[h], b, 0], w4(src[tok[h], 0:W4]),
                                                        ALU.subtract).then_inc(ut_done, 1)
                    Ru = R[:].rearrange("p h (b c) d -> p h b c d", b=B)
                    for c in range(NCH):
                        dve.wait_ge(dl_ready, n * NCH + c + 1)
                        nc.vector.tensor_copy(Ru[tok[1], 1, :, c, :], w4(IA[0][tok[1], 0:W4])).then_inc(dl_done, 1)
                        if c < NCH - 1:
                            dve.wait_ge(st_ready, n * (NCH - 1) + c + 1)
                            nc.vector.tensor_copy(Ru[dk[1], 1, :, c + 1, :], w4(IB[0][dk[1], 0:W4])).then_inc(st_done, 1)
                        if c % 2:
                            t = c // 2
                            base = n * 8 + 4 * t
                            dve.wait_ge(osq_done, n * 2 + t + 1)
                            nc.vector.tensor_reduce(ost[:, 0, :], sqo[:], AX.X, ALU.add).then_inc(ost_step, 1)
                            dve.wait_ge(ost_step, base + 1)
                            qst = qs[:].rearrange("p (b t) h -> p b t h", t=2)[:, :, t, :]
                            nc.vector.scalar_tensor_tensor(out=ost[:, 1, :].rearrange("p (b h) -> p b h", h=2), in0=ost[:, 0, :].rearrange("p (b h) -> p b h", h=2),
                                                           scalar=1.0 / D, in1=qst, op0=ALU.mult, op1=ALU.add).then_inc(ost_step, 1)
                            dve.wait_ge(rms_done, n * 2 + t + 1)
                            nc.vector.tensor_tensor(on[:], OB[:].rearrange("p (b d) -> p b d", d=D), over(ost[:, 2, :]), ALU.mult).then_inc(ost_step, 1)
                            dve.wait_ge(ost_step, base + 3)
                            ztt = zt[:].rearrange("p (b t) m -> p b t m", t=2)[:, :, t, :]
                            if t:
                                dve.wait_ge(ogT_ready, n * 2 + 1)
                            nc.vector.scalar_tensor_tensor(out=og[:], in0=ztt, scalar=1.0, in1=on[:].rearrange("p (b h) d -> p b (h d)", h=2),
                                                           op0=ALU.add, op1=ALU.mult).then_inc(og_done, 1)
                            nc.vector.tensor_copy(ost[:, 0, 0:1], ost[:, 2, 0:1]).then_inc(ost_step, 1)


def finish(nc, sem, sb, bank, oT, yffn, nw, wout, x, out):
    with ExitStack() as ctx:
        xr = sb("xr", [TT, HID], F32, ctx)
        y = sb("y", [TT, HID], F32, ctx)
        woutT = sb("woutT", [PAIRS, HID], F32, ctx)
        nwc = sb("nwc", [1], F32, ctx)
        wout_in, wout_done = sem("wout_in"), sem("wout_done")
        x2_in, xy_done, op_ready, op_used, out_done = (sem(n) for n in ("x2_in", "xy_done", "op_ready", "op_used", "out_done"))
        with nc.Block() as block:
            @block.sync
            def _(sp):
                sp.dma_start(woutT[:], wout).then_inc(wout_in, 16)
                for h in range(2):
                    sp.dma_start(nwc[h * C:h * C + C, :], nw).then_inc(wout_in, 16)
                sp.dma_start(xr[:], x.rearrange("(t p) d -> p t d", p=P)).then_inc(x2_in, 16)
                for t in range(TT):
                    sp.wait_ge(op_used, t + 1)
                    sp.dma_start(out.rearrange("(t p) d -> p t d", p=P)[:, t, :], y[:, t, :]).then_inc(out_done, 16)
                sp.wait_ge(out_done, 16 * TT)

            @block.tensor
            def _(pe):
                pe.wait_ge(wout_done, 1)
                for t in range(TT):
                    for h in range(PAIRS):
                        last = nc.tensor.matmul(bank[t][:, 0:HID], oT[:, h, t * P:t * P + P], woutT[:, h, :], start=h == 0, stop=h == PAIRS - 1)
                    last.then_inc(op_ready, 1)

            @block.vector
            def _(dve):
                dve.wait_ge(wout_in, 48)
                nc.vector.tensor_scalar(woutT[:], woutT[:], nwc[:, 0:1], 0.5, ALU.mult, ALU.mult).then_inc(wout_done, 1)
                dve.wait_ge(x2_in, 16)
                nc.vector.tensor_tensor(xr[:], xr[:], yffn[:], ALU.add).then_inc(xy_done, 1)
                dve.wait_ge(xy_done, 1)
                for t in range(TT):
                    dve.wait_ge(op_ready, t + 1)
                    nc.vector.tensor_tensor(y[:, t, :], bank[t][:, 0:HID], xr[:, t, :], ALU.add).then_inc(op_used, 1)


def kernel(L0_attn_hidden_states, L0_attn_w_qkvz, L0_attn_w_ba, L0_attn_conv_w, L0_attn_A_log, L0_attn_dt_bias,
           L0_attn_norm_weight, L0_attn_w_out, L0_ffn_SU_ug, L0_ffn_SU_dp, L0_ffn_Wscale_ug, L0_ffn_Wscale_dp,
           L0_ffn_W_up, L0_ffn_W_gate, L0_ffn_W_down):
    import concourse.bacc as bacc
    from concourse.bass_utils import run_bass_kernel_spmd

    def lay(a):
        return np.ascontiguousarray(a)

    a = np.asarray
    w = a(L0_attn_w_qkvz).reshape(PAIRS, 2, 4, D, KC, P)[:, :, [1, 0, 2, 3]].transpose(0, 5, 4, 2, 1, 3).reshape(PAIRS, P, KC, 4, P)
    ba = a(L0_attn_w_ba).reshape(PAIRS, 2, 2, KC, P)[:, ::-1].transpose(4, 3, 1, 2, 0).reshape(P, KC, 2, 2 * PAIRS)
    cv = a(L0_attn_conv_w).reshape(3, PAIRS, P, 4)[[1, 0, 2]].transpose(1, 2, 0, 3)
    arrays = {
        "x": lay(a(L0_attn_hidden_states).reshape(NTOK, HID)),
        "wqkvz": lay(w), "wba": lay(ba), "conv": lay(cv),
        "alog": lay(a(L0_attn_A_log).reshape(PAIRS, 2).T), "dtb": lay(a(L0_attn_dt_bias).reshape(PAIRS, 2).T),
        "nw": lay(a(L0_attn_norm_weight).reshape(D, 1)),
        "wout": lay(a(L0_attn_w_out).reshape(HID, PAIRS, P).transpose(2, 1, 0)),
        "su_ug": lay(a(L0_ffn_SU_ug).reshape(KC, P).T), "su_dp": lay(a(L0_ffn_SU_dp).reshape(IT, P).T),
        "ws_up": lay(a(L0_ffn_Wscale_ug)[:INTER].reshape(IT, P).T), "ws_gate": lay(a(L0_ffn_Wscale_ug)[INTER:].reshape(IT, P).T),
        "ws_dp": lay(a(L0_ffn_Wscale_dp).reshape(1, HID)),
        "wup": lay(a(L0_ffn_W_up).reshape(INTER, KC, P).transpose(2, 1, 0)),
        "wgate": lay(a(L0_ffn_W_gate).reshape(INTER, KC, P).transpose(2, 1, 0)),
        "wdown": lay(a(L0_ffn_W_down).reshape(HID, IT, P).transpose(2, 1, 0)),
        "consts": constants(),
    }
    nc = bacc.Bacc("TRN2", target_bir_lowering=False, num_devices=1)
    args = [nc.dram_tensor(f"{n}_dram", v.shape, mybir.dt.from_np(v.dtype), kind="ExternalInput").ap() for n, v in arrays.items()]
    out = nc.dram_tensor("out_dram", (NTOK, HID), F32, kind="ExternalOutput").ap()
    build(nc, *args, out)
    r = run_bass_kernel_spmd(nc, [{f"{n}_dram": v for n, v in arrays.items()}], core_ids=[0])
    return r.results[0]["out_dram"].reshape(B, S, HID)
```

```python
from contextlib import ExitStack

import numpy as np

import concourse.bass as bass
from concourse import mybir
from concourse.alu_op_type import AluOpType as ALU

F32 = mybir.dt.float32
BF16 = mybir.dt.bfloat16
ACT = mybir.ActivationFunctionType
AX = mybir.AxisListType

P = 128
B, S, HID = 4, 256, 256
NH, D = 32, 64
NTOK = B * S
KC = HID // P
PAIRS = NH // 2
C = 64
NCH = S // C
UNITS = B * NCH
TT = NTOK // P
INTER = 1024
IT = INTER // P
BASE = 16
EPS = 1e-6
LN_EPS = 1e-5
GATE_FLOOR = -104.0

CONST = {}
_at = 0
for _name, _n in (("ident", P), ("eye", C), ("cum", C), ("strict_bd", P), ("cum_bd", P), ("swap", P),
                  ("neg", C), ("one", 1), ("hsel", 2), ("base", C), ("base_d", C), ("merge", C), ("diag", BASE),
                  ("tinit", BASE), ("sel", BASE * P), ("had", P), ("half", UNITS), ("neghalf", UNITS)):
    CONST[_name] = (_at, _at + _n)
    _at += _n
NCONST = _at


def constants():
    c = np.zeros((P, NCONST), np.float32)

    def put(name, x):
        c[:, CONST[name][0]:CONST[name][1]] = x

    r, i = np.arange(P)[:, None], np.arange(C)[None, :]
    cc = np.arange(P)[None, :]
    j = r % C
    put("ident", r == cc)
    put("eye", j == i)
    put("cum", j <= i)
    put("strict_bd", (r // C == cc // C) & (r % C > cc % C))
    put("cum_bd", (r // C == cc // C) & (r % C <= cc % C))
    put("swap", r // C != cc // C)
    put("neg", np.where(j > i, -1e30, 0.0))
    put("one", 1.0)
    put("hsel", r // C == np.arange(2)[None, :])
    same = j // BASE == i // BASE
    put("base", same & (j < i))
    put("base_d", same)
    put("merge", (j // (2 * BASE) == i // (2 * BASE)) & (j // BASE < i // BASE))
    m = np.arange(BASE)[None, :]
    put("diag", r % BASE == m)
    put("tinit", np.where(r % BASE == m, np.where(m == 0, 1.0, -1.0), 0.0))
    put("sel", np.concatenate([(r // BASE == cc // BASE) & (r % BASE == row) for row in range(BASE)], axis=1))
    bits = np.array([[bin(a & b).count("1") % 2 for b in range(P)] for a in range(P)])
    put("had", 1.0 - 2.0 * bits)
    put("half", 0.5)
    put("neghalf", -0.5)
    return c


def build(nc, x, wqkvz, wba, conv, alog, dtb, nw, wout, su_ug, su_dp, ws_up, ws_gate, ws_dp,
          wup, wgate, wdown, consts, out):
    with ExitStack() as keep:
        def sb(name, shape, dt=F32, ctx=keep):
            return ctx.enter_context(nc.sbuf_tensor(name, [P] + shape, dt))

        def sem(name):
            return keep.enter_context(nc.semaphore(name))

        bank = [keep.enter_context(nc.psum_tensor(f"bank{i}", [P, 512], F32)) for i in range(8)]
        cst = sb("cst", [NCONST])

        def k(name):
            return cst[:, CONST[name][0]:CONST[name][1]]

        xnT = sb("xnT", [KC, NTOK])
        scal = sb("scal", [PAIRS, 4, UNITS])
        negb = sb("negb", [C], BF16)
        identb = sb("identb", [P], BF16)
        yacc = sb("yacc", [TT, HID])

        setup_and_ffn(nc, sem, sb, bank, k, cst, xnT, scal, negb, identb, yacc,
                      x, wba, alog, dtb, su_ug, su_dp, ws_up, ws_gate, ws_dp,
                      wup, wgate, wdown, consts)
        attention(nc, sem, sb, bank, k, xnT, scal, negb, identb, yacc, wqkvz, conv, wout, nw)
        finish(nc, sem, yacc, out)


def setup_and_ffn(nc, sem, sb, bank, k, cst, xnT, scal, negb, identb, yacc,
                  x, wba, alog, dtb, su_ug, su_dp, ws_up, ws_gate, ws_dp,
                  wup, wgate, wdown, consts):
    with ExitStack() as ctx:
        def tmp(name, shape, dt=F32):
            return sb(name, shape, dt, ctx)

        xs = tmp("xs", [TT, HID])
        xc = tmp("xc", [TT, HID])
        xq = tmp("xq", [TT, HID])
        st = tmp("st", [4, TT])
        wbas = tmp("wbas", [KC, 2, 2 * PAIRS])
        ah = tmp("ah", [3, PAIRS])
        ga = tmp("ga", [8, PAIRS, UNITS])
        vec = tmp("vec", [KC + 3 * IT])
        wsd = tmp("wsd", [HID])
        wupT = tmp("wupT", [KC, INTER])
        wgaT = tmp("wgaT", [KC, INTER])
        wdT = tmp("wdT", [2, IT, HID])
        hug = tmp("hug", [KC, KC, P])
        xh = tmp("xh", [KC, NTOK])
        hT = tmp("hT", [IT, NTOK])
        th = tmp("th", [2, 512])
        gl = tmp("gl", [2, 512])
        coef = tmp("coef", [2, IT])
        su, sd, wsu, wsg = (vec[:, a:a + n] for a, n in ((0, KC), (KC, IT), (KC + IT, IT), (KC + 2 * IT, IT)))

        x_in, const_in, gate_in, ffn_in = (sem(n) for n in ("x_in", "const_in", "gate_in", "ffn_in"))
        v_step, xnT_ready, xnT_used = sem("v_step"), sem("xnT_ready"), sem("xnT_used")
        ba_ready, a_step, cum_ready = sem("ba_ready"), sem("a_step"), sem("cum_ready")
        hug_made, xh_ready, xh_done = sem("hug_made"), sem("xh_ready"), sem("xh_done")
        wd_ready, wd_used, wd_done = sem("wd_ready"), sem("wd_used"), sem("wd_done")
        gu_ready, tanh_done, gu_used = sem("gu_ready"), sem("tanh_done"), sem("gu_used")
        y_ready, y_done = sem("y_ready"), sem("y_done")
        rstd_done = sem("rstd_done")
        steps = {}

        with nc.Block() as block:
            @block.sync
            def _(sp):
                sp.dma_start(xs[:], x.rearrange("(t p) d -> p t d", p=P)).then_inc(x_in, 16)
                sp.dma_start(yacc[:], x.rearrange("(t p) d -> p t d", p=P)).then_inc(x_in, 16)
                sp.dma_start(cst[:], consts).then_inc(const_in, 16)
                sp.dma_start(wbas[:], wba).then_inc(gate_in, 16)
                for h in range(2):
                    rows = slice(h * C, h * C + C)
                    for m, src in enumerate((alog, dtb)):
                        sp.dma_start(ah[rows, m, :], src[1 - h:2 - h, :].broadcast_to([C, PAIRS])).then_inc(gate_in, 16)
                sp.dma_start(wdT[:, 0, :, :], wdown).then_inc(ffn_in, 16)
                for v, src in ((su, su_ug), (sd, su_dp), (wsu, ws_up), (wsg, ws_gate)):
                    sp.dma_start(v, src).then_inc(ffn_in, 16)
                sp.dma_start(wsd[:], ws_dp.broadcast_to([P, HID])).then_inc(ffn_in, 16)
                sp.dma_start(wupT[:], wup).then_inc(ffn_in, 16)
                sp.dma_start(wgaT[:], wgate).then_inc(ffn_in, 16)

            NFFN = 16 * 8

            @block.vector
            def _(dve):
                count = [0]

                def step(ins):
                    count[0] += 1
                    ins.then_inc(v_step, 1)
                    dve.wait_ge(v_step, count[0])

                def over(a, n):
                    return a.unsqueeze(2).broadcast_to([P, TT, n])

                dve.wait_ge(x_in, 32)
                step(nc.vector.tensor_reduce(st[:, 0, :], xs[:], AX.X, ALU.add))
                step(nc.vector.tensor_scalar(st[:, 1, :], st[:, 0, :], 1.0 / HID, None, ALU.mult))
                step(nc.vector.tensor_tensor(xc[:], xs[:], over(st[:, 1, :], HID), ALU.subtract))
                step(nc.vector.tensor_tensor(xq[:], xc[:], xc[:], ALU.mult))
                step(nc.vector.tensor_reduce(st[:, 2, :], xq[:], AX.X, ALU.add))
                step(nc.vector.tensor_scalar(st[:, 0, :], st[:, 2, :], 1.0 / HID, LN_EPS, ALU.mult, ALU.add))
                steps["var"] = count[0]
                dve.wait_ge(rstd_done, 1)
                step(nc.vector.tensor_tensor(xs[:], xc[:], over(st[:, 3, :], HID), ALU.mult))
                steps["xn"] = count[0]
                dve.wait_ge(const_in, 16)
                step(nc.vector.tensor_copy(negb[:], k("neg")))
                step(nc.vector.tensor_copy(identb[:], k("ident")))
                for q in range(1, 4, 2):
                    dve.wait_ge(xnT_ready, q + 1)
                    nc.vector.tensor_copy(xnT[:, q // 2, (q % 2) * 512:(q % 2) * 512 + 512], bank[q][:]).then_inc(xnT_used, 1)
                dve.wait_ge(ffn_in, NFFN)
                for kc in range(KC):
                    for mc in range(KC):
                        sign = (1.0 if not (kc and mc) else -1.0) / float(np.sqrt(HID))
                        nc.vector.tensor_scalar(hug[:, kc, mc, :], k("had"), su[:, kc:kc + 1], sign, ALU.mult, ALU.mult)\
                          .then_inc(hug_made, 1)
                step(nc.vector.tensor_tensor(coef[:, 0, :], wsg, wsu, ALU.mult))
                step(nc.vector.scalar_tensor_tensor(out=coef[:, 1, :], in0=coef[:, 0, :], scalar=0.5, in1=sd, op0=ALU.mult, op1=ALU.mult))
                step(nc.vector.tensor_scalar(coef[:, 0, :], wsg, 0.5, None, ALU.mult))
                steps["coef"] = count[0]
                dve.wait_ge(ba_ready, 1)
                step(nc.vector.tensor_copy(ga[:, 0:2, :, :].rearrange("p k h u -> p u k h"),
                                           bank[4][:].rearrange("p (u k h) -> p u k h", u=UNITS, k=2)))
                steps["ba"] = count[0]
                gb = lambda a: a.unsqueeze(2).broadcast_to([P, PAIRS, UNITS])
                step(nc.vector.tensor_tensor(ga[:, 2, :, :], ga[:, 1, :, :], gb(ah[:, 1, :]), ALU.add))
                step(nc.vector.scalar_tensor_tensor(out=ga[:, 3, :, :], in0=ga[:, 2, :, :], scalar=-1.0, in1=ga[:, 2, :, :],
                                                    op0=ALU.mult, op1=ALU.max))
                steps["abs"] = count[0]
                step(nc.vector.tensor_scalar(ga[:, 2, :, :], ga[:, 2, :, :], 0.0, None, ALU.max))
                dve.wait_ge(a_step, 2)
                step(nc.vector.tensor_scalar(ga[:, 0, :, :], ga[:, 4, :, :], 1.0, None, ALU.add))
                step(nc.vector.reciprocal(scal[:, :, 1, :], ga[:, 0, :, :]))
                dve.wait_ge(a_step, 3)
                step(nc.vector.tensor_scalar(ga[:, 0, :, :], ga[:, 5, :, :], 2.0, None, ALU.add))
                step(nc.vector.reciprocal(ga[:, 6, :, :], ga[:, 0, :, :]))
                step(nc.vector.tensor_tensor(ga[:, 0, :, :], ga[:, 5, :, :], ga[:, 6, :, :], ALU.mult))
                step(nc.vector.tensor_tensor(ga[:, 1, :, :], ga[:, 0, :, :], ga[:, 0, :, :], ALU.mult))
                step(nc.vector.tensor_scalar(ga[:, 6, :, :], ga[:, 1, :, :], 1.0 / 17, 1.0 / 15, ALU.mult, ALU.add))
                for m in (13, 11, 9, 7, 5, 3, 1):
                    step(nc.vector.tensor_tensor(ga[:, 6, :, :], ga[:, 6, :, :], ga[:, 1, :, :], ALU.mult))
                    step(nc.vector.tensor_scalar(ga[:, 6, :, :], ga[:, 6, :, :], 1.0 / m, None, ALU.add))
                step(nc.vector.tensor_tensor(ga[:, 6, :, :], ga[:, 6, :, :], ga[:, 0, :, :], ALU.mult))
                step(nc.vector.scalar_tensor_tensor(out=ga[:, 6, :, :], in0=ga[:, 6, :, :], scalar=2.0, in1=ga[:, 2, :, :],
                                                    op0=ALU.mult, op1=ALU.add))
                step(nc.vector.tensor_scalar(ah[:, 2, :], ah[:, 0, :], -1.0, None, ALU.mult))
                step(nc.vector.tensor_tensor(ga[:, 7, :, :], ga[:, 6, :, :], gb(ah[:, 2, :]), ALU.mult))
                step(nc.vector.tensor_scalar(scal[:, :, 0, :], ga[:, 7, :, :], GATE_FLOOR, None, ALU.max))
                step(nc.vector.tensor_scalar(ga[:, 7, :, :], ga[:, 7, :, :], GATE_FLOOR, None, ALU.max))
                steps["g"] = count[0]
                dve.wait_ge(wd_used, 4)
                for h in (1, 2, 4):
                    src, dst = (wdT[:, 1], wdT[:, 0]) if h != 2 else (wdT[:, 0], wdT[:, 1])
                    s4 = src.rearrange("p (a t h) d -> p a t (h d)", t=2, h=h)
                    d4 = dst.rearrange("p (a t h) d -> p a t (h d)", t=2, h=h)
                    nc.vector.tensor_tensor(d4[:, :, 0], s4[:, :, 0], s4[:, :, 1], ALU.add)
                    step(nc.vector.tensor_tensor(d4[:, :, 1], s4[:, :, 0], s4[:, :, 1], ALU.subtract))
                nc.vector.scalar_tensor_tensor(
                    out=wdT[:, 1], in0=wdT[:, 0], scalar=1.0 / float(np.sqrt(INTER)),
                    in1=wsd[:].unsqueeze(1).broadcast_to([P, IT, HID]), op0=ALU.mult, op1=ALU.mult).then_inc(wd_done, 1)
                for n in range(2 * IT):
                    i, t = n // 2, n % 2
                    dve.wait_ge(tanh_done, n + 1)
                    g, u = bank[2 * (n % 2)], bank[2 * (n % 2) + 1]
                    step(nc.vector.scalar_tensor_tensor(out=gl[:, n % 2, :], in0=th[:, n % 2, :], scalar=1.0, in1=g[:],
                                                        op0=ALU.add, op1=ALU.mult))
                    nc.vector.scalar_tensor_tensor(out=hT[:, i, t * 512:t * 512 + 512], in0=u[:], scalar=coef[:, 1, i:i + 1],
                                                   in1=gl[:, n % 2, :], op0=ALU.mult, op1=ALU.mult).then_inc(gu_used, 1)
                for t in range(0, TT, 2):
                    dve.wait_ge(y_ready, t // 2 + 1)
                    nc.vector.tensor_tensor(yacc[:, t:t + 2, :], yacc[:, t:t + 2, :], bank[4 + (t // 2) % 2][:].rearrange("p (t d) -> p t d", t=2), ALU.add)\
                      .then_inc(y_done, 1)

            @block.gpsimd
            def _(pool):
                pool.wait_ge(const_in, 16)
                pool.wait_ge(v_step, steps["var"])
                nc.gpsimd.tensor_tensor(st[:, 3, :], st[:, 0, :], k("neghalf")[:, 0:TT], ALU.pow).then_inc(rstd_done, 1)

            @block.scalar
            def _(act):
                for q in range(0, 4, 2):
                    act.wait_ge(xnT_ready, q + 1)
                    nc.scalar.activation(xnT[:, q // 2, 0:512], bank[q][:], ACT.Copy).then_inc(xnT_used, 1)
                act.wait_ge(gate_in, 16 * 5)
                nc.scalar.activation(ah[:, 0, :], ah[:, 0, :], ACT.Exp).then_inc(a_step, 1)
                act.wait_ge(v_step, steps["ba"])
                nc.scalar.activation(ga[:, 4, :, :], ga[:, 0, :, :], ACT.Exp, scale=-1.0).then_inc(a_step, 1)
                act.wait_ge(v_step, steps["abs"])
                nc.scalar.activation(ga[:, 5, :, :], ga[:, 3, :, :], ACT.Exp, scale=-1.0).then_inc(a_step, 1)
                for m in range(KC * 2):
                    act.wait_ge(xh_ready, m + 1)
                    nc.scalar.activation(xh[:, m // 2, (m % 2) * 512:(m % 2) * 512 + 512], bank[m][:], ACT.Copy).then_inc(xh_done, 1)
                for m in range(4):
                    act.wait_ge(wd_ready, m + 1)
                    nc.scalar.activation(wdT[:, 1, 2 * m:2 * m + 2, :], bank[4 + m][:].rearrange("p (t d) -> p t d", t=2), ACT.Copy)\
                      .then_inc(wd_used, 1)
                act.wait_ge(cum_ready, 1)
                for m in range(2):
                    nc.scalar.activation(scal[:, :, 2 + m, :], bank[5][:, m * 256:m * 256 + 256].rearrange("p (h u) -> p h u", h=PAIRS),
                                         ACT.Exp).then_inc(a_step, 1)
                act.wait_ge(v_step, steps["coef"])
                for n in range(2 * IT):
                    act.wait_ge(gu_ready, n + 1)
                    if n >= 2:
                        act.wait_ge(gu_used, n - 1)
                    nc.scalar.activation(th[:, n % 2, :], bank[2 * (n % 2)][:], ACT.Tanh, scale=coef[:, 0, n // 2:n // 2 + 1]).then_inc(tanh_done, 1)

            @block.tensor
            def _(pe):
                pe.wait_ge(const_in, 16)
                pe.wait_ge(v_step, steps["xn"])
                for q in range(4):
                    kc, t0 = q // 2, 4 * (q % 2)
                    for t in range(4):
                        last = nc.tensor.transpose(bank[q][:, t * P:t * P + P], xs[:, t0 + t, kc * P:kc * P + P], k("ident"))
                    last.then_inc(xnT_ready, 1)
                pe.wait_ge(xnT_used, 4)
                pe.wait_ge(gate_in, 16 * 5)
                for u in range(UNITS):
                    for h in range(2):
                        first = (u // NCH) * S + (u + h) % NCH * C
                        for kc in range(KC):
                            last = nc.tensor.matmul(bank[4][h * C:h * C + C, u * 2 * PAIRS:(u + 1) * 2 * PAIRS],
                                                    xnT[:, kc, first:first + C], wbas[:, kc, h, :], start=kc == 0, stop=kc == KC - 1)
                last.then_inc(ba_ready, 1)
                pe.wait_ge(hug_made, 4)
                for m in range(KC * 2):
                    for kc in range(KC):
                        last = nc.tensor.matmul(bank[m][:], hug[:, kc, m // 2, :], xnT[:, kc, (m % 2) * 512:(m % 2) * 512 + 512],
                                                start=kc == 0, stop=kc == KC - 1)
                    last.then_inc(xh_ready, 1)
                pe.wait_ge(v_step, steps["ba"])
                pe.wait_ge(ffn_in, NFFN)
                for m in range(4):
                    nc.tensor.matmul(bank[4 + m][:], k("had"), wdT[:, 0, 2 * m:2 * m + 2, :], start=True, stop=True).then_inc(wd_ready, 1)
                pe.wait_ge(wd_used, 4)
                pe.wait_ge(v_step, steps["g"])
                nc.tensor.matmul(bank[5][:, 0:256], k("cum_bd"), ga[:, 7, :, :], start=True, stop=True)
                nc.tensor.matmul(bank[5][:, 256:512], k("strict_bd"), ga[:, 7, :, :], start=True, stop=True).then_inc(cum_ready, 1)
                pe.wait_ge(xh_done, 4)
                for n in range(2 * IT):
                    i, t = n // 2, n % 2
                    if n >= 2:
                        pe.wait_ge(gu_used, n - 1)
                    for w, dst in ((wgaT, bank[2 * (n % 2)]), (wupT, bank[2 * (n % 2) + 1])):
                        for kc in range(KC):
                            last = nc.tensor.matmul(dst[:], w[:, kc, i * P:i * P + P], xh[:, kc, t * 512:t * 512 + 512],
                                                    start=kc == 0, stop=kc == KC - 1)
                    last.then_inc(gu_ready, 1)
                pe.wait_ge(gu_used, 2 * IT)
                pe.wait_ge(wd_done, 1)
                pe.wait_ge(a_step, 5)
                for t in range(TT):
                    if t % 2 == 0 and t >= 4:
                        pe.wait_ge(y_done, t // 2 - 1)
                    for i in range(IT):
                        last = nc.tensor.matmul(bank[4 + (t // 2) % 2][:, (t % 2) * HID:(t % 2) * HID + HID],
                                                hT[:, i, t * P:t * P + P], wdT[:, 1, i, :], start=i == 0, stop=i == IT - 1)
                    if t % 2:
                        last.then_inc(y_ready, 1)


def attention(nc, sem, sb, bank, k, xnT, scal, negb, identb, yacc, wqkvz, conv, wout, nw):
    with ExitStack() as ctx:
        def tmp(name, shape, dt=F32):
            return sb(name, shape, dt, ctx)

        W4 = NCH * C
        SW = S + C
        NB = BASE
        cw = tmp("cw", [2, 3, 4])
        sc = tmp("sc", [2, 4, UNITS])
        woraw = tmp("woraw", [HID])
        wo = tmp("wo", [2, HID])
        zt = tmp("zt", [2, TT, P])
        AT = tmp("AT", [2, B, NCH, C])
        ME = tmp("ME", [2, B, NCH, C])
        X = tmp("X", [UNITS, NB])
        kg = tmp("kg", [2, B, NCH, C])
        LBo = tmp("LBo", [2, 2, UNITS, C])
        LBs = tmp("LBs", [2, 2, UNITS, C])
        R = tmp("R", [2, 2, UNITS, C])
        qs = tmp("qs", [2, TT, 2])
        wq = tmp("wq", [KC, 4, P])
        nwh = tmp("nwh", [1])
        kq = tmp("kq", [3, B, SW])
        sqq = tmp("sqq", [2, 2, SW])
        gm = tmp("gm", [2, NCH, C])
        gg = tmp("gg", [2, 2, NCH, C])
        gb_ = tmp("gb", [2, NCH, C])
        stat = tmp("stat", [6, UNITS])
        Xt = tmp("Xt", [2, NCH, C // NB + 1, NB])
        kc_ = tmp("kc", [2, NCH, C])
        XT = tmp("XT", [UNITS, NB])
        Tb = tmp("Tb", [UNITS, NB])
        prod = tmp("prod", [UNITS, NB])
        UT = tmp("UT", [B, 2, NCH, C])
        ET = tmp("ET", [2, NCH, C])
        EH = tmp("EH", [2, NCH, C // 2])
        LA = tmp("LA", [2, UNITS, C])
        sqo = tmp("sqo", [B * 2, D])
        ost = tmp("ost", [3, B * 2])
        og = tmp("og", [B, P])
        oTs = tmp("oTs", [2, B, P])

        names = """w_in cw_in sc_in wo_in nw_in wo_done proj_done tap0_done conv_step z_done wrap_done gm_done dg_done gexp_done
                   gram_done scale_step root_done gb_done at_done pt_done x_prod x_done me_done trk_done kc_done trv_done v_done
                   kg_done lb_done sqq_done qst_done qs_done s0_zero tinit_done xt_ready xt_done sel_ready base_step t16_ready
                   tx_done u16_ready u16_done et_ready et_done up_ready up_done eh_ready eh_done lc_done hb_ready la_done w_ready
                   w_done dl_ready dl_done st_ready st_done o_ready osq_done ms_step ms_done rms_done on_done og_done ogT_ready
                   ogT_done op_ready acc_done nwh_done turn pool_turn""".split()
        sems = {x: sem(x) for x in names}
        (w_in, cw_in, sc_in, wo_in, nw_in, wo_done, proj_done, tap0_done, conv_step, z_done, wrap_done, gm_done, dg_done, gexp_done,
         gram_done, scale_step, root_done, gb_done, at_done, pt_done, x_prod, x_done, me_done, trk_done, kc_done, trv_done, v_done,
         kg_done, lb_done, sqq_done, qst_done, qs_done, s0_zero, tinit_done, xt_ready, xt_done, sel_ready, base_step, t16_ready,
         tx_done, u16_ready, u16_done, et_ready, et_done, up_ready, up_done, eh_ready, eh_done, lc_done, hb_ready, la_done, w_ready,
         w_done, dl_ready, dl_done, st_ready, st_done, o_ready, osq_done, ms_step, ms_done, rms_done, on_done, og_done, ogT_ready,
         ogT_done, op_ready, acc_done, nwh_done, turn, pool_turn) = (sems[x] for x in names)

        ring = [bank[0], bank[1]]
        DG, GR, TR = bank[2], bank[3], bank[4]
        XY, Z = [bank[5], bank[6]], bank[7]
        tok, dk = (slice(C, P), slice(0, C)), (slice(0, C), slice(C, P))
        H2 = C // 2
        top = tuple(slice(t.start, t.start + H2) for t in tok)
        low = tuple(slice(t.start + H2, t.start + C) for t in tok)

        NBLK = 2 * (P // NB)
        loads, free = [[]], 512
        for i in range(1, NB):
            if free < NBLK * (i + 1):
                loads.append([])
                free = 512
            loads[-1].append((i, 512 - free))
            free -= NBLK * (i + 1)
        NLOAD = len(loads)

        def slot(h, c):
            return (c - 1) % NCH if h == 0 else c

        def cols(h, w):
            a = (w + (h == 0)) * C
            return slice(a, a + C)

        def w4(ap, n=NCH):
            return ap.rearrange("p (u c) -> p u c", u=n)

        def over(a, n=C):
            return a.unsqueeze(2).broadcast_to([a.shape[0], a.shape[1], n])

        def each(a, n=NCH):
            return a.unsqueeze(1).broadcast_to([a.shape[0], n, a.shape[1]])

        def us(b):
            return slice(b * NCH, (b + 1) * NCH)

        body = """A.load A.proj.0 A.proj.1 A.proj.2 A.wrap.0 M.t16 A.ksq.0 M.u.0 M.u.1 M.u.2 A.gate.0 A.gram.0 M.u.3 M.ea.0 A.at.0
                  A.val.0 A.proj.3 M.ea.1 M.eb.0 A.x.0 M.ea.2 A.gate.1 A.gram.1 A.at.1 A.val.1 A.proj.4 M.eb.1 A.x.1 A.proj.5 M.ea.3
                  M.eb.2 M.eb.3 M.ha.0 M.ha.1 A.wrap.1 M.hb.0 M.ha.2 M.hb.1 A.ksq.1 A.proj.6 A.gate.2 A.gram.2 A.at.2 M.ha.3 M.hb.2
                  M.hb.3 M.w.0 A.val.2 M.w.1 M.w.2 M.w.3 A.x.2 A.gate.3 M.delta.0 A.gram.3 A.at.3 M.state.0 M.delta.1 A.val.3 M.state.1
                  M.norm.0 A.proj.7 A.x.3 A.xt M.delta.2 M.gated.0 A.sel.0 M.state.2 A.sel.1 M.turn.0 M.delta.3 A.sel.2 M.state.3
                  M.norm.1 M.out.0 M.gated.1 A.sel.3 A.sel.4 M.turn.1 M.out.1""".split()
        assert NLOAD == 5

        def steps(do, kinds, n, q):
            for step in body:
                kind, name, *number = step.split(".")
                if kind in kinds and name in do:
                    do[name](*((n, q) if kind == "M" else (n + 1, 1 - q)), *map(int, number))

        def program(eng, do):
            steps(do, "A", -1, 1)
            with eng.Fori(0, PAIRS - 2, 2) as n:
                steps(do, "AM", n, 0)
                steps(do, "AM", n + 1, 1)
            steps(do, "AM", PAIRS - 2, 0)
            steps(do, "M", PAIRS - 1, 1)

        def wait(eng, sm, value):
            if not isinstance(value, int) or value > 0:
                eng.wait_ge(sm, value)

        with nc.Block() as block:
            @block.sync
            def _(sp):
                def load(m, q):
                    wait(sp, proj_done, m * 8)
                    src = (lambda t: t[bass.ds(m, 1)]) if not isinstance(m, int) else (lambda t: t[m:m + 1])
                    sp.dma_start(wq[:], src(wqkvz).rearrange("o p c t m -> (o p) c t m")).then_inc(w_in, 16)
                    wait(sp, conv_step, m * 18)
                    sp.dma_start(cw[:, q], src(conv).rearrange("o p t m -> (o p) t m")).then_inc(cw_in, 16)
                    wait(sp, wo_done, m)
                    sp.dma_start(woraw[:], src(wout).rearrange("o p m -> (o p) m")).then_inc(wo_in, 16)
                    wait(sp, lb_done, m * 6 * B)
                    sl = slice(m, m + 1) if isinstance(m, int) else bass.ds(m, 1)
                    sp.dma_start(sc[:, q], scal[:, sl].rearrange("p o k u -> p (o k) u")).then_inc(sc_in, 16)

                for h in range(2):
                    sp.dma_start(nwh[h * C:h * C + C, :], nw).then_inc(nw_in, 16)
                program(sp, {"load": load})

            @block.tensor
            def _(pe):
                def alone():
                    pe.sem_inc(turn, 1)

                def proj(m, q, i):
                    if i == 0:
                        pe.wait_ge(w_in, (m + 1) * 16)
                        wait(pe, base_step, m * 2 * (NB - 1))
                    if i >= 2:
                        pe.wait_ge(conv_step, m * 18 + 3 * (i - 1))
                    dst = ring[i % 2]
                    if i < 6:
                        for kc in range(KC):
                            last = nc.tensor.matmul(dst[:], wq[:, kc, i % 3, :], xnT[:, kc, (i // 3) * 512:(i // 3) * 512 + 512],
                                                    start=kc == 0, stop=kc == KC - 1)
                    else:
                        for t in range(4):
                            tt = 4 * (i - 6) + t
                            for kc in range(KC):
                                last = nc.tensor.matmul(dst[:, t * P:t * P + P], xnT[:, kc, tt * P:tt * P + P], wq[:, kc, 3, :],
                                                        start=kc == 0, stop=kc == KC - 1)
                    last.then_inc(proj_done, 1)

                def turned(m, b, which, done):
                    for w in range(NCH):
                        last = nc.tensor.transpose(TR[:, w * P:w * P + P], kq[:, which, b, w * C:w * C + P], k("ident"))
                    last.then_inc(done, 1)

                def gate(m, q, b):
                    g = m * B + b
                    pe.wait_ge(gm_done, g + 1)
                    wait(pe, gexp_done, g)
                    nc.tensor.matmul(DG[:, 0:W4], k("strict_bd"), gm[:, b % 2], start=True, stop=False)
                    nc.tensor.matmul(DG[:, 0:W4], identb[:], each(negb[:]), start=False, stop=True)
                    nc.tensor.matmul(DG[:, W4:2 * W4], k("swap"), gm[:, b % 2], start=True, stop=True).then_inc(dg_done, 1)
                    pe.wait_ge(wrap_done, m * 2 + b // 2 + 1)
                    if b % 2 == 0:
                        pe.wait_ge(qs_done, m * 2 + b // 2 + 1)
                    else:
                        pe.wait_ge(v_done, 2 * g)
                    turned(m, b, 0, trk_done)

                def gram(m, q, b):
                    g = m * B + b
                    pe.wait_ge(wrap_done, m * 2 + b // 2 + 1)
                    wait(pe, pt_done, 2 * g)
                    alone()
                    for w in range(NCH):
                        for h in range(2):
                            last = nc.tensor.matmul(GR[tok[h], w * P:w * P + P], kq[dk[h], 0, b, cols(h, w)], kq[dk[h], 0:2, b, cols(h, w)],
                                                    start=True, stop=True)
                    last.then_inc(gram_done, 1)

                def val(m, q, b):
                    pe.wait_ge(kc_done, 2 * (m * B + b) + 2)
                    turned(m, b, 2, trv_done)

                def ksq(m, q, j):
                    pe.wait_ge(sqq_done, m * 2 + j + 1)
                    if j == 0:
                        wait(pe, xt_done, m)
                    else:
                        pe.wait_ge(v_done, (m * 2 + 1) * B)
                    alone()
                    for r in range(2):
                        for w in range(NCH):
                            for h in range(2):
                                at = r * NCH + w
                                nc.tensor.matmul(TR[tok[h], at:at + 1], sqq[dk[h], 0, r, cols(h, w)], k("one")[dk[h]], start=True, stop=True)
                    for t in range(4):
                        at = 2 * NCH + 2 * t
                        last = nc.tensor.matmul(TR[:, at:at + 2], sqq[:, 1, t // 2, (t % 2) * P:(t % 2) * P + P], k("hsel"), start=True, stop=True)
                    last.then_inc(qst_done, 1)

                def xt(m, q):
                    pe.wait_ge(x_done, m * B + B)
                    pe.wait_ge(v_done, (m + 1) * 2 * B)
                    for z in range(2):
                        last = nc.tensor.transpose(TR[:, z * P:z * P + P], X[:, z * 8:z * 8 + 8, :].rearrange("p u c -> p (u c)"), k("ident"))
                    last.then_inc(xt_ready, 1)

                def sel(m, q, g):
                    if g == 0:
                        pe.wait_ge(xt_done, m + 1)
                        pe.wait_ge(z_done, (m + 1) * 2)
                    if g >= 2:
                        pe.wait_ge(base_step, m * 2 * (NB - 1) + 2 * loads[g - 2][-1][0] - 1)
                    for i, at in loads[g]:
                        last = nc.tensor.matmul(ring[g % 2][:, at:at + NBLK * (i + 1)], k("sel")[:, i * P:i * P + P], XT[:, :, 0:i + 1],
                                                start=True, stop=True)
                    last.then_inc(sel_ready, 1)

                def t16(n, q):
                    pe.wait_ge(base_step, (n + 1) * 2 * (NB - 1))
                    pe.wait_ge(on_done, n * 2 + 1)
                    for z in range(2):
                        last = nc.tensor.transpose(Z[:, z * P:z * P + P], Tb[:, z * 8:z * 8 + 8, :].rearrange("p u c -> p (u c)"), k("ident"))
                    last.then_inc(t16_ready, 1)

                def u(n, q, b):
                    pe.wait_ge(tx_done, n * B + b + 1)
                    if b >= 2:
                        pe.wait_ge(u16_done, n * B + b - 1)
                    elif b == 0:
                        pe.wait_ge(acc_done, n * 4 + 1)
                    alone()
                    for w in range(NCH):
                        for h in range(2):
                            last = nc.tensor.matmul(XY[b % 2][tok[h], w * C:w * C + C], UT[tok[h], b, 1, w, :], k("eye")[tok[h]], start=True, stop=True)
                    last.then_inc(u16_ready, 1)

                def ea(n, q, b):
                    pe.wait_ge(me_done, n * B + b + 1)
                    if b:
                        pe.wait_ge(et_done, n * B + b)
                    else:
                        pe.wait_ge(tx_done, n * B + B)
                    alone()
                    for w in range(NCH):
                        for h in range(2):
                            last = nc.tensor.matmul(Z[tok[h], w * C:w * C + C], ME[tok[h], q, b, w, :], UT[tok[h], b, 1, w, :], start=True, stop=True)
                    last.then_inc(et_ready, 1)

                def eb(n, q, b):
                    pe.wait_ge(et_done, n * B + b + 1)
                    if b < 2:
                        pe.wait_ge(u16_done, n * B + b + 3)
                    else:
                        pe.wait_ge(up_done, n * B + b - 1)
                    alone()
                    for w in range(NCH):
                        for h in range(2):
                            nc.tensor.matmul(XY[b % 2][tok[h], w * C:w * C + C], ET[tok[h], b % 2, w, :], UT[tok[h], b, 0, w, :], start=True, stop=True)
                            last = nc.tensor.matmul(XY[b % 2][tok[h], W4 + w * C:W4 + w * C + C], UT[tok[h], b, 0, w, :], ET[tok[h], b % 2, w, :],
                                                    start=True, stop=True)
                    last.then_inc(up_ready, 1)

                def ha(n, q, b):
                    pe.wait_ge(up_done, n * B + b + 1)
                    if b:
                        pe.wait_ge(eh_done, n * B + b)
                    else:
                        pe.wait_ge(et_done, n * B + B)
                    alone()
                    for w in range(NCH):
                        for h in range(2):
                            last = nc.tensor.matmul(Z[low[h], w * H2:w * H2 + H2], AT[top[h], q, b, w, H2:C], UT[top[h], b, 1, w, 0:H2], start=True, stop=True)
                    last.then_inc(eh_ready, 1)

                def hb(n, q, b):
                    pe.wait_ge(eh_done, n * B + b + 1)
                    if b < 2:
                        pe.wait_ge(up_done, n * B + b + 3)
                    else:
                        pe.wait_ge(la_done, 2 * (n * B + b - 1))
                    alone()
                    for w in range(NCH):
                        for h in range(2):
                            last = nc.tensor.matmul(XY[b % 2][top[h], w * H2:w * H2 + H2], EH[low[h], b % 2, w, :], UT[low[h], b, 0, w, H2:C],
                                                    start=True, stop=True)
                    last.then_inc(hb_ready, 1)

                def w(n, q, b):
                    pe.wait_ge(la_done, 2 * (n * B + b) + 2)
                    pe.wait_ge(kg_done, n * B + b + 1)
                    if b:
                        pe.wait_ge(w_done, 2 * (n * B + b))
                    else:
                        pe.wait_ge(eh_done, n * B + B)
                    alone()
                    for v in range(NCH):
                        for h in range(2):
                            last = nc.tensor.matmul(Z[dk[h], v * C:v * C + C], kg[tok[h], q, b, v, :], LA[tok[h], h, b * NCH + v, :], start=True, stop=True)
                    last.then_inc(w_ready, 1)

                def delta(n, q, c):
                    if c == 0:
                        pe.wait_ge(w_done, 2 * (n * B + B))
                        pe.wait_ge(la_done, 2 * (n * B + B))
                    else:
                        pe.wait_ge(st_done, 2 * (n * (NCH - 1) + c))
                    if c == 3:
                        pe.wait_ge(ogT_done, n * 2 + 1)
                    for b in range(B):
                        for h in range(2):
                            v = b * NCH + slot(h, c)
                            last = nc.tensor.matmul(XY[0][tok[h], b * C:b * C + C], LA[:, h, v, :], R[:, q, h, v, :], start=True, stop=True)
                    last.then_inc(dl_ready, 1)

                def state(n, q, c):
                    pe.wait_ge(dl_done, 2 * (n * NCH + c) + 2)
                    if c == 0:
                        pe.wait_ge(lb_done, (n + 1) * 6 * B)
                    if c < NCH - 1:
                        for b in range(B):
                            for h in range(2):
                                v = b * NCH + slot(h, c)
                                last = nc.tensor.matmul(XY[1][dk[h], b * C:b * C + C], LBs[:, q, h, v, :], R[:, q, h, v, :], start=True, stop=True)
                        last.then_inc(st_ready, 1)
                    if c == 2:
                        pe.wait_ge(on_done, n * 2 + 2)
                    for b in range(B):
                        for h in range(2):
                            v = b * NCH + slot(h, c)
                            r = (c % 2) * C
                            last = nc.tensor.matmul(Z[r:r + C, b * P + h * C:b * P + h * C + C], LBo[:, q, h, v, :], R[:, q, h, v, :],
                                                    start=True, stop=True)
                    last.then_inc(o_ready, 1)

                def turn_(n, q, t):
                    pe.wait_ge(og_done, n * 2 + t + 1)
                    if t:
                        pe.wait_ge(acc_done, n * 4 + 3)
                    else:
                        pe.wait_ge(dl_done, 2 * (n * NCH + 3))
                    for b in range(B):
                        last = nc.tensor.transpose(XY[0][:, b * P:b * P + P], og[:, b, :], k("ident"))
                    last.then_inc(ogT_ready, 1)

                def out(n, q, t):
                    pe.wait_ge(ogT_done, n * 2 + t + 1)
                    pe.wait_ge(wo_done, n + 1)
                    if t:
                        pe.wait_ge(acc_done, n * 4 + 2)
                    else:
                        pe.wait_ge(dl_done, 2 * (n * NCH + NCH))
                    for j in range(2):
                        for b in range(2 * j, 2 * j + 2):
                            last = nc.tensor.matmul(XY[1 - j][:, (b % 2) * HID:(b % 2) * HID + HID], oTs[:, t, b, :], wo[:, q, :], start=True, stop=True)
                        last.then_inc(op_ready, 1)

                pe.wait_ge(s0_zero, 1)
                program(pe, {"proj": proj, "gate": gate, "gram": gram, "val": val, "ksq": ksq, "xt": xt, "sel": sel, "t16": t16, "u": u,
                             "ea": ea, "eb": eb, "ha": ha, "hb": hb, "w": w, "delta": delta, "state": state, "turn": turn_, "out": out})

            @block.scalar
            def _(act):
                def proj(m, q, i):
                    act.wait_ge(proj_done, m * 8 + i + 1)
                    if i < 6:
                        if i == 0:
                            act.wait_ge(cw_in, (m + 1) * 16)
                            wait(act, gram_done, m * B)
                            wait(act, trv_done, m * B)
                            wait(act, lb_done, m * 6 * B)
                        nc.scalar.activation(kq[:, i % 3, 2 * (i // 3):2 * (i // 3) + 2, 0:S], w4(ring[i % 2][:], 2), ACT.Copy,
                                             scale=cw[:, q, i % 3, 3:4]).then_inc(tap0_done, 1)
                    else:
                        nc.scalar.activation(zt[:, q, 4 * (i - 6):4 * (i - 6) + 4, :], w4(ring[i % 2][:], 4), ACT.Tanh, scale=0.5).then_inc(z_done, 1)
                    if i == 7:
                        act.wait_ge(wo_in, (m + 1) * 16)
                        nc.scalar.activation(wo[:, q], woraw[:], ACT.Copy, scale=nwh[:]).then_inc(wo_done, 1)

                def gate(m, q, b):
                    g = m * B + b
                    act.wait_ge(dg_done, g + 1)
                    wait(act, lb_done, 6 * (g - 1))
                    nc.scalar.activation(gg[:, b % 2], DG[:].rearrange("p (k u c) -> p k u c", k=2, u=NCH), ACT.Exp).then_inc(gexp_done, 1)
                    act.wait_ge(trk_done, g + 1)
                    for h in range(2):
                        nc.scalar.activation(kc_[tok[h], b % 2], w4(TR[:])[tok[h], :, h * C:h * C + C], ACT.Copy).then_inc(kc_done, 1)

                def ksq(m, q, j):
                    act.wait_ge(wrap_done, m * 2 + j + 1)
                    wait(act, qst_done, m * 2 + j)
                    nc.scalar.activation(sqq[:], kq[:, 0:2, 2 * j:2 * j + 2, :], ACT.Square).then_inc(sqq_done, 1)

                def xt(m, q):
                    act.wait_ge(xt_ready, m + 1)
                    nc.scalar.activation(XT[:], w4(TR[:, 0:UNITS * NB], UNITS), ACT.Copy).then_inc(xt_done, 1)

                def u(n, q, b):
                    act.wait_ge(u16_ready, n * B + b + 1)
                    nc.scalar.activation(UT[:, b, 0], w4(XY[b % 2][:, 0:W4]), ACT.Copy).then_inc(u16_done, 1)

                def ea(n, q, b):
                    act.wait_ge(et_ready, n * B + b + 1)
                    if b >= 2:
                        act.wait_ge(up_ready, n * B + b - 1)
                    nc.scalar.activation(ET[:, b % 2], w4(Z[:, 0:W4]), ACT.Copy).then_inc(et_done, 1)

                def ha(n, q, b):
                    act.wait_ge(up_done, n * B + b + 1)
                    for h in range(2):
                        nc.scalar.activation(LA[tok[h], h, us(b), :], UT[tok[h], b, 0], ACT.Copy).then_inc(lc_done, 1)
                    act.wait_ge(eh_ready, n * B + b + 1)
                    if b >= 2:
                        act.wait_ge(hb_ready, n * B + b - 1)
                    nc.scalar.activation(EH[:, b % 2], w4(Z[:, 0:NCH * H2]), ACT.Copy).then_inc(eh_done, 1)

                def w(n, q, b):
                    act.wait_ge(w_ready, n * B + b + 1)
                    for h in range(2):
                        nc.scalar.activation(LA[dk[h], h, us(b), :], w4(Z[dk[h], 0:W4]), ACT.Copy, scale=-1.0).then_inc(w_done, 1)

                def delta(n, q, c):
                    act.wait_ge(dl_ready, n * NCH + c + 1)
                    dst = R[tok[0], q, 0].rearrange("p (b c) d -> p b c d", b=B)[:, :, slot(0, c), :]
                    nc.scalar.activation(dst, w4(XY[0][tok[0], 0:W4]), ACT.Copy).then_inc(dl_done, 1)

                def state(n, q, c):
                    if c < NCH - 1:
                        act.wait_ge(st_ready, n * (NCH - 1) + c + 1)
                        dst = R[dk[0], q, 0].rearrange("p (b c) d -> p b c d", b=B)[:, :, slot(0, c + 1), :]
                        nc.scalar.activation(dst, w4(XY[1][dk[0], 0:W4]), ACT.Copy).then_inc(st_done, 1)

                def norm(n, q, t):
                    act.wait_ge(o_ready, n * NCH + 2 * t + 2)
                    if t:
                        act.wait_ge(ms_step, n * 2 + 1)
                    nc.scalar.activation(sqo[:], Z[:].rearrange("p (b d) -> p b d", d=D), ACT.Square).then_inc(osq_done, 1)

                def turn_(n, q, t):
                    act.wait_ge(ogT_ready, n * 2 + t + 1)
                    nc.scalar.activation(oTs[:, t], w4(XY[0][:], B), ACT.Copy).then_inc(ogT_done, 1)

                act.wait_ge(nw_in, 32)
                nc.scalar.activation(nwh[:], nwh[:], ACT.Copy, scale=0.5).then_inc(nwh_done, 1)
                act.wait_ge(nwh_done, 1)
                program(act, {"proj": proj, "gate": gate, "ksq": ksq, "xt": xt, "u": u, "ea": ea, "ha": ha, "w": w,
                              "delta": delta, "state": state, "norm": norm, "turn": turn_})

            @block.gpsimd
            def _(pool):
                def alone():
                    pool.sem_inc(pool_turn, 1)

                def wrap(m, q, j):
                    pool.wait_ge(conv_step, m * 18 + 9 * (j + 1))
                    rows = slice(2 * j, 2 * j + 2)
                    alone()
                    nc.gpsimd.tensor_copy(kq[:, :, rows, S:SW], kq[:, :, rows, 0:C]).then_inc(wrap_done, 1)

                def gate(m, q, b):
                    g = m * B + b
                    if b == 0:
                        pool.wait_ge(sc_in, (m + 1) * 16)
                    wait(pool, dg_done, g - 1)
                    nc.gpsimd.tensor_tensor(gm[:, b % 2], over(sc[:, q, 0, us(b)]), each(k("cum")), ALU.mult).then_inc(gm_done, 1)

                def ksq(m, q, j):
                    pool.wait_ge(scale_step, 4 * (m * 2 + j) + 1)
                    wait(pool, v_done, 4 * (m * 2 + j) - 4)
                    rows = slice(2 * j * NCH, (2 * j + 2) * NCH)
                    nc.gpsimd.tensor_tensor(stat[:, 2, rows], stat[:, 5, rows], k("half")[:, rows], ALU.pow).then_inc(root_done, 1)

                def gram(m, q, b):
                    g = m * B + b
                    pool.wait_ge(gexp_done, g + 1)
                    pool.wait_ge(scale_step, 4 * (m * 2 + b // 2) + 3)
                    wait(pool, pt_done, 2 * (g - 1))
                    nc.gpsimd.tensor_tensor(gb_[:, b % 2], gg[:, b % 2, 0], over(stat[:, 3, us(b)]), ALU.mult).then_inc(gb_done, 1)
                    pool.wait_ge(kc_done, 2 * g + 2)
                    nc.gpsimd.tensor_tensor(kg[:, q, b], kc_[:, b % 2], over(sc[:, q, 2, us(b)]), ALU.mult).then_inc(kg_done, 1)

                def val(m, q, b):
                    g = m * B + b
                    pool.wait_ge(at_done, g + 1)
                    wait(pool, x_done, g - 1)
                    nc.gpsimd.tensor_tensor(Xt[:, b % 2, :, 0:C // NB, :], AT[:, q, b].rearrange("p u (k c) -> p u k c", c=NB),
                                            each(k("base")).rearrange("p u (k c) -> p u k c", c=NB), ALU.mult).then_inc(x_prod, 1)
                    nc.gpsimd.tensor_tensor(ME[:, q, b], AT[:, q, b], each(k("merge")), ALU.mult).then_inc(me_done, 1)
                    pool.wait_ge(me_done, g + 1)
                    pool.wait_ge(scale_step, 4 * (m * 2 + b // 2) + 4)
                    for half in range(2):
                        hq, hk = (0, 1) if half == 0 else (1, 0)
                        if half:
                            pool.wait_ge(lb_done, 6 * g + 3)
                        nc.gpsimd.tensor_tensor(LBo[dk[hq], q, hq, us(b), :], w4(kq[dk[hq], 1, b, (1 - hq) * C:(1 - hq) * C + S]),
                                                gg[dk[hq], b % 2, 1], ALU.mult).then_inc(lb_done, 1)
                        nc.gpsimd.tensor_tensor(LBs[dk[hq], q, hq, us(b), :], each(k("eye")[dk[hq]]),
                                                gg[dk[hq], b % 2, 1, :, C - 1:C].broadcast_to([C, NCH, C]), ALU.mult).then_inc(lb_done, 1)
                        nc.gpsimd.tensor_tensor(LBs[tok[hk], q, hk, us(b), :], kc_[tok[hk], b % 2], over(stat[tok[hk], 4, us(b)]), ALU.mult)\
                          .then_inc(lb_done, 1)
                    pool.wait_ge(lb_done, 6 * g + 6)

                def xt(m, q):
                    wait(pool, t16_ready, m)
                    alone()
                    nc.gpsimd.tensor_copy(Tb[:], each(k("tinit"), UNITS)).then_inc(tinit_done, 1)

                def norm(n, q, t):
                    pool.wait_ge(ms_done, n * 2 + t + 1)
                    nc.gpsimd.tensor_tensor(ost[:, 2, :], ost[:, 1, :], k("neghalf")[:, 0:B * 2], ALU.pow).then_inc(rms_done, 1)

                nc.gpsimd.memset(R[:], 0.0).then_inc(s0_zero, 1)
                for j in range(2):
                    nc.gpsimd.tensor_copy(Xt[:, j, :, C // NB, :], each(k("diag"))).then_inc(s0_zero, 1)
                program(pool, {"wrap": wrap, "ksq": ksq, "gate": gate, "gram": gram, "val": val, "xt": xt, "norm": norm})

            @block.vector
            def _(dve):
                def proj(m, q, i):
                    if i >= 6:
                        return
                    y = kq[:, i % 3, 2 * (i // 3):2 * (i // 3) + 2, :]
                    p = w4(ring[i % 2][:], 2)
                    dve.wait_ge(tap0_done, m * 6 + i + 1)
                    for t in (1, 2, 3):
                        nc.vector.scalar_tensor_tensor(out=y[:, :, t:S], in0=p[:, :, 0:S - t], scalar=cw[:, q, i % 3, 3 - t:4 - t],
                                                       in1=y[:, :, t:S], op0=ALU.mult, op1=ALU.add).then_inc(conv_step, 1)
                        dve.wait_ge(conv_step, m * 18 + 3 * i + t)

                def ksq(m, q, j):
                    base = 4 * (m * 2 + j)
                    rows = slice(2 * j * NCH, (2 * j + 2) * NCH)
                    dve.wait_ge(qst_done, m * 2 + j + 1)
                    wait(dve, lb_done, 6 * (m * B + 2 * j - 2))
                    nc.vector.tensor_scalar(stat[:, 5, rows], TR[:, 0:2 * NCH], EPS, None, ALU.add).then_inc(scale_step, 1)
                    nc.vector.tensor_scalar(qs[:, q, 4 * j:4 * j + 4], TR[:, 2 * NCH:2 * NCH + 8].rearrange("p (t h) -> p t h", h=2),
                                            EPS, EPS * D, ALU.add, ALU.mult).then_inc(qs_done, 1)
                    dve.wait_ge(scale_step, base + 1)
                    nc.vector.reciprocal(stat[:, 1, rows], stat[:, 5, rows]).then_inc(scale_step, 1)
                    dve.wait_ge(scale_step, base + 2)
                    if j == 0:
                        dve.wait_ge(sc_in, (m + 1) * 16)
                    nc.vector.tensor_tensor(stat[:, 3, rows], stat[:, 1, rows], sc[:, q, 1, rows], ALU.mult).then_inc(scale_step, 1)
                    dve.wait_ge(scale_step, base + 3)
                    nc.vector.tensor_tensor(stat[:, 4, rows], stat[:, 3, rows], sc[:, q, 3, rows], ALU.mult).then_inc(scale_step, 1)

                def at(m, q, b):
                    g = m * B + b
                    gr = GR[:].rearrange("p (u k c) -> p u k c", u=NCH, k=2)
                    dve.wait_ge(gram_done, g + 1)
                    dve.wait_ge(gb_done, g + 1)
                    nc.vector.tensor_tensor(AT[:, q, b], gr[:, :, 0, :], gb_[:, b % 2], ALU.mult).then_inc(at_done, 1)
                    for h in range(2):
                        nc.vector.tensor_tensor(LBo[tok[h], q, h, us(b), :], gr[tok[h], :, 1, :], gb_[tok[h], b % 2], ALU.mult).then_inc(pt_done, 1)

                def val(m, q, b):
                    g = m * B + b
                    dve.wait_ge(trv_done, g + 1)
                    dve.wait_ge(root_done, m * 2 + b // 2 + 1)
                    for h in range(2):
                        nc.vector.tensor_tensor(R[tok[h], q, h, us(b), :], w4(TR[:])[tok[h], :, h * C:h * C + C], over(stat[tok[h], 2, us(b)]),
                                                ALU.mult).then_inc(v_done, 1)

                def x(m, q, b):
                    dve.wait_ge(x_prod, m * B + b + 1)
                    if b == 0:
                        wait(dve, xt_ready, m)
                    nc.vector.tensor_reduce(X[:, us(b), :], Xt[:, b % 2].rearrange("p u k c -> p u c k"), AX.X, ALU.add).then_inc(x_done, 1)

                def sel(m, q, g):
                    if g == 0:
                        dve.wait_ge(tinit_done, m + 1)
                    dve.wait_ge(sel_ready, m * NLOAD + g + 1)
                    for i, at in loads[g]:
                        base = m * 2 * (NB - 1) + 2 * (i - 1)
                        if i > 1:
                            dve.wait_ge(base_step, base)
                        nc.vector.tensor_tensor(prod[:, :, 0:i + 1], w4(ring[g % 2][:, at:at + NBLK * (i + 1)], NBLK), Tb[:, :, 0:i + 1], ALU.mult)\
                          .then_inc(base_step, 1)
                        dve.wait_ge(base_step, base + 1)
                        nc.vector.tensor_reduce(Tb[:, :, i], prod[:, :, 0:i + 1], AX.X, ALU.add, negate=True).then_inc(base_step, 1)

                def t16(n, q):
                    dve.wait_ge(t16_ready, n + 1)
                    for b in range(B):
                        src = w4(Z[:, b * NCH * NB:(b + 1) * NCH * NB]).unsqueeze(2).broadcast_to([P, NCH, C // NB, NB])
                        nc.vector.tensor_tensor(UT[:, b, 1].rearrange("p u (k c) -> p u k c", c=NB), src,
                                                each(k("base_d")).rearrange("p u (k c) -> p u k c", c=NB), ALU.mult).then_inc(tx_done, 1)

                def eb(n, q, b):
                    dve.wait_ge(up_ready, n * B + b + 1)
                    nc.vector.tensor_tensor(UT[:, b], UT[:, b], XY[b % 2][:].rearrange("p (k u c) -> p k u c", k=2, u=NCH), ALU.subtract).then_inc(up_done, 1)

                def hb(n, q, b):
                    dve.wait_ge(hb_ready, n * B + b + 1)
                    dve.wait_ge(lc_done, 2 * (n * B + b) + 2)
                    for h in range(2):
                        nc.vector.tensor_scalar(LA[top[h], h, us(b), H2:C], w4(XY[b % 2][top[h], 0:NCH * H2]), -1.0, None, ALU.mult).then_inc(la_done, 1)

                def delta(n, q, c):
                    dve.wait_ge(dl_ready, n * NCH + c + 1)
                    dst = R[tok[1], q, 1].rearrange("p (b c) d -> p b c d", b=B)[:, :, slot(1, c), :]
                    nc.vector.tensor_copy(dst, w4(XY[0][tok[1], 0:W4])).then_inc(dl_done, 1)

                def state(n, q, c):
                    if c < NCH - 1:
                        dve.wait_ge(st_ready, n * (NCH - 1) + c + 1)
                        dst = R[dk[1], q, 1].rearrange("p (b c) d -> p b c d", b=B)[:, :, slot(1, c + 1), :]
                        nc.vector.tensor_copy(dst, w4(XY[1][dk[1], 0:W4])).then_inc(st_done, 1)

                def norm(n, q, t):
                    dve.wait_ge(osq_done, n * 2 + t + 1)
                    nc.vector.tensor_reduce(ost[:, 0, :], sqo[:], AX.X, ALU.add).then_inc(ms_step, 1)
                    dve.wait_ge(ms_step, n * 2 + t + 1)
                    h2 = lambda a: a.rearrange("p (b h) -> p b h", h=2)
                    nc.vector.scalar_tensor_tensor(out=h2(ost[:, 1, :]), in0=h2(ost[:, 0, :]), scalar=1.0 / D,
                                                   in1=qs[:, q].rearrange("p (b t) h -> p b t h", t=2)[:, :, t, :], op0=ALU.mult, op1=ALU.add).then_inc(ms_done, 1)

                def gated(n, q, t):
                    dve.wait_ge(rms_done, n * 2 + t + 1)
                    if t:
                        dve.wait_ge(ogT_ready, n * 2 + 1)
                    o = og[:].rearrange("p b (h d) -> p (b h) d", h=2)
                    nc.vector.tensor_tensor(o, Z[:].rearrange("p (b d) -> p b d", d=D), over(ost[:, 2, :]), ALU.mult).then_inc(on_done, 1)
                    dve.wait_ge(on_done, n * 2 + t + 2)
                    nc.vector.scalar_tensor_tensor(out=og[:], in0=zt[:, q].rearrange("p (b t) m -> p b t m", t=2)[:, :, t, :], scalar=1.0, in1=og[:],
                                                   op0=ALU.add, op1=ALU.mult).then_inc(og_done, 1)

                def out(n, q, t):
                    for j in range(2):
                        dve.wait_ge(op_ready, n * 4 + 2 * t + j + 1)
                        y = yacc[:].rearrange("p (b t) m -> p b t m", t=2)[:, 2 * j:2 * j + 2, t, :]
                        nc.vector.tensor_tensor(y, y, w4(XY[1 - j][:], 2), ALU.add).then_inc(acc_done, 1)

                dve.wait_ge(s0_zero, 3)
                dve.sem_inc(on_done, 1)
                dve.sem_inc(acc_done, 1)
                program(dve, {"proj": proj, "ksq": ksq, "at": at, "val": val, "x": x, "sel": sel, "t16": t16, "eb": eb, "hb": hb,
                              "delta": delta, "state": state, "norm": norm, "gated": gated, "out": out})


def finish(nc, sem, yacc, out):
    out_done = sem("out_done")
    with nc.Block() as block:
        @block.sync
        def _(sp):
            sp.dma_start(out.rearrange("(t p) d -> p t d", p=P), yacc[:]).then_inc(out_done, 16)
            sp.wait_ge(out_done, 16)


def kernel(L0_attn_hidden_states, L0_attn_w_qkvz, L0_attn_w_ba, L0_attn_conv_w, L0_attn_A_log, L0_attn_dt_bias,
           L0_attn_norm_weight, L0_attn_w_out, L0_ffn_SU_ug, L0_ffn_SU_dp, L0_ffn_Wscale_ug, L0_ffn_Wscale_dp,
           L0_ffn_W_up, L0_ffn_W_gate, L0_ffn_W_down):
    import concourse.bacc as bacc
    from concourse.bass_utils import run_bass_kernel_spmd

    def lay(a):
        return np.ascontiguousarray(a)

    a = np.asarray
    w = a(L0_attn_w_qkvz).reshape(PAIRS, 2, 4, D, KC, P)[:, :, [1, 0, 2, 3]].transpose(0, 5, 4, 2, 1, 3).reshape(PAIRS, P, KC, 4, P)
    ba = a(L0_attn_w_ba).reshape(PAIRS, 2, 2, KC, P)[:, ::-1].transpose(4, 3, 1, 2, 0).reshape(P, KC, 2, 2 * PAIRS)
    cv = a(L0_attn_conv_w).reshape(3, PAIRS, P, 4)[[1, 0, 2]].transpose(1, 2, 0, 3)
    arrays = {
        "x": lay(a(L0_attn_hidden_states).reshape(NTOK, HID)),
        "wqkvz": lay(w), "wba": lay(ba), "conv": lay(cv),
        "alog": lay(a(L0_attn_A_log).reshape(PAIRS, 2).T), "dtb": lay(a(L0_attn_dt_bias).reshape(PAIRS, 2).T),
        "nw": lay(a(L0_attn_norm_weight).reshape(D, 1)),
        "wout": lay(a(L0_attn_w_out).reshape(HID, PAIRS, P).transpose(1, 2, 0)),
        "su_ug": lay(a(L0_ffn_SU_ug).reshape(KC, P).T), "su_dp": lay(a(L0_ffn_SU_dp).reshape(IT, P).T),
        "ws_up": lay(a(L0_ffn_Wscale_ug)[:INTER].reshape(IT, P).T), "ws_gate": lay(a(L0_ffn_Wscale_ug)[INTER:].reshape(IT, P).T),
        "ws_dp": lay(a(L0_ffn_Wscale_dp).reshape(1, HID)),
        "wup": lay(a(L0_ffn_W_up).reshape(INTER, KC, P).transpose(2, 1, 0)),
        "wgate": lay(a(L0_ffn_W_gate).reshape(INTER, KC, P).transpose(2, 1, 0)),
        "wdown": lay(a(L0_ffn_W_down).reshape(HID, IT, P).transpose(2, 1, 0)),
        "consts": constants(),
    }
    nc = bacc.Bacc("TRN2", target_bir_lowering=False, num_devices=1)
    args = [nc.dram_tensor(f"{n}_dram", v.shape, mybir.dt.from_np(v.dtype), kind="ExternalInput").ap() for n, v in arrays.items()]
    out = nc.dram_tensor("out_dram", (NTOK, HID), F32, kind="ExternalOutput").ap()
    build(nc, *args, out)
    r = run_bass_kernel_spmd(nc, [{f"{n}_dram": v for n, v in arrays.items()}], core_ids=[0])
    return r.results[0]["out_dram"].reshape(B, S, HID)
```

```python
from contextlib import ExitStack

import numpy as np

import concourse.bass as bass
from concourse import mybir
from concourse.alu_op_type import AluOpType as ALU

F32 = mybir.dt.float32
BF16 = mybir.dt.bfloat16
ACT = mybir.ActivationFunctionType
AX = mybir.AxisListType

P = 128
B, S, HID = 4, 256, 256
NH, D = 32, 64
NTOK = B * S
KC = HID // P
PAIRS = NH // 2
C = 64
NCH = S // C
UNITS = B * NCH
TT = NTOK // P
INTER = 1024
IT = INTER // P
BASE = 16
EPS = 1e-6
LN_EPS = 1e-5
GATE_FLOOR = -104.0

CONST = {}
_at = 0
for _name, _n in (("ident", P), ("eye", C), ("cum", C), ("strict_bd", P), ("cum_bd", P), ("swap", P),
                  ("neg", C), ("hsel", 2), ("base", C), ("base_d", C), ("merge", C), ("diag", BASE),
                  ("tinit", BASE), ("sel", BASE * P), ("had", P), ("half", UNITS), ("neghalf", UNITS)):
    CONST[_name] = (_at, _at + _n)
    _at += _n
NCONST = _at


def constants():
    c = np.zeros((P, NCONST), np.float32)

    def put(name, x):
        c[:, CONST[name][0]:CONST[name][1]] = x

    r, i = np.arange(P)[:, None], np.arange(C)[None, :]
    cc = np.arange(P)[None, :]
    j = r % C
    put("ident", r == cc)
    put("eye", j == i)
    put("cum", j <= i)
    put("strict_bd", (r // C == cc // C) & (r % C > cc % C))
    put("cum_bd", (r // C == cc // C) & (r % C <= cc % C))
    put("swap", r // C != cc // C)
    put("neg", np.where(j > i, -1e30, 0.0))
    put("hsel", r // C == np.arange(2)[None, :])
    same = j // BASE == i // BASE
    put("base", same & (j < i))
    put("base_d", same)
    put("merge", (j // (2 * BASE) == i // (2 * BASE)) & (j // BASE < i // BASE))
    m = np.arange(BASE)[None, :]
    put("diag", r % BASE == m)
    put("tinit", np.where(r % BASE == m, np.where(m == 0, 1.0, -1.0), 0.0))
    put("sel", np.concatenate([(r // BASE == cc // BASE) & (r % BASE == row) for row in range(BASE)], axis=1))
    bits = np.array([[bin(a & b).count("1") % 2 for b in range(P)] for a in range(P)])
    put("had", 1.0 - 2.0 * bits)
    put("half", 0.5)
    put("neghalf", -0.5)
    return c


def build(nc, x, wqkvz, wba, conv, alog, dtb, nw, wout, su_ug, su_dp, ws_up, ws_gate, ws_dp,
          wgu, wdown, consts, out):
    with ExitStack() as keep:
        def sb(name, shape, dt=F32, ctx=keep):
            return ctx.enter_context(nc.sbuf_tensor(name, [P] + shape, dt))

        def sem(name):
            return keep.enter_context(nc.semaphore(name))

        bank = [keep.enter_context(nc.psum_tensor(f"bank{i}", [P, 512], F32)) for i in range(8)]
        cst = sb("cst", [NCONST])

        def k(name):
            return cst[:, CONST[name][0]:CONST[name][1]]

        xnT = sb("xnT", [KC, NTOK])
        scal = sb("scal", [PAIRS, 4, UNITS])
        negb = sb("negb", [C], BF16)
        identb = sb("identb", [P], BF16)
        yacc = sb("yacc", [TT, HID])
        xh = sb("xh", [KC, NTOK])
        wdf = sb("wdf", [2 * IT, HID // 2])
        coef = sb("coef", [2 * IT])

        setup(nc, sem, sb, bank, k, cst, xnT, scal, negb, identb, yacc, xh, wdf, coef,
              x, wba, alog, dtb, su_ug, su_dp, ws_up, ws_gate, ws_dp, wdown, consts)
        pairs(nc, sem, sb, bank, k, xnT, scal, negb, identb, yacc, xh, wdf, coef, wqkvz, conv, wout, nw, wgu)
        finish(nc, sem, yacc, out)


def setup(nc, sem, sb, bank, k, cst, xnT, scal, negb, identb, yacc, xh, wdf, coef,
          x, wba, alog, dtb, su_ug, su_dp, ws_up, ws_gate, ws_dp, wdown, consts):
    with ExitStack() as ctx:
        def tmp(name, shape, dt=F32):
            return sb(name, shape, dt, ctx)

        xs = tmp("xs", [TT, HID])
        xc = tmp("xc", [TT, HID])
        xq = tmp("xq", [TT, HID])
        st = tmp("st", [4, TT])
        wbas = tmp("wbas", [KC, 2, 2 * PAIRS])
        ah = tmp("ah", [3, PAIRS])
        ga = tmp("ga", [8, PAIRS, UNITS])
        vec = tmp("vec", [KC + 3 * IT])
        wsd = tmp("wsd", [HID])
        wdT = tmp("wdT", [2, IT, HID])
        hug = tmp("hug", [KC, KC, P])
        su, sd, wsu, wsg = (vec[:, a:a + n] for a, n in ((0, KC), (KC, IT), (KC + IT, IT), (KC + 2 * IT, IT)))

        x_in, res_in, const_in, gate_in, ffn_in = (sem(n) for n in ("x_in", "res_in", "const_in", "gate_in", "ffn_in"))
        v_step, xnT_ready, xnT_used = sem("v_step"), sem("xnT_ready"), sem("xnT_used")
        ba_ready, a_step, cum_ready = sem("ba_ready"), sem("a_step"), sem("cum_ready")
        hug_made, xh_ready, xh_done = sem("hug_made"), sem("xh_ready"), sem("xh_done")
        wd_ready, wd_used, wd_done = sem("wd_ready"), sem("wd_used"), sem("wd_done")
        rstd_done = sem("rstd_done")
        steps = {}

        with nc.Block() as block:
            @block.sync
            def _(sp):
                sp.dma_start(xs[:], x.rearrange("(t p) d -> p t d", p=P)).then_inc(x_in, 16)
                sp.dma_start(cst[:], consts).then_inc(const_in, 16)
                sp.dma_start(wbas[:], wba).then_inc(gate_in, 16)
                for h in range(2):
                    rows = slice(h * C, h * C + C)
                    for m, src in enumerate((alog, dtb)):
                        sp.dma_start(ah[rows, m, :], src[1 - h:2 - h, :].broadcast_to([C, PAIRS])).then_inc(gate_in, 16)
                sp.dma_start(wdT[:, 0, :, :], wdown).then_inc(ffn_in, 16)
                for v, src in ((su, su_ug), (sd, su_dp), (wsu, ws_up), (wsg, ws_gate)):
                    sp.dma_start(v, src).then_inc(ffn_in, 16)
                sp.dma_start(wsd[:], ws_dp.broadcast_to([P, HID])).then_inc(ffn_in, 16)
                sp.dma_start(yacc[:], x.rearrange("(t p) d -> p t d", p=P)).then_inc(res_in, 16)

            NFFN = 16 * 6

            @block.vector
            def _(dve):
                count = [0]

                def step(ins):
                    count[0] += 1
                    ins.then_inc(v_step, 1)
                    dve.wait_ge(v_step, count[0])

                def over(a, n):
                    return a.unsqueeze(2).broadcast_to([P, TT, n])

                dve.wait_ge(x_in, 16)
                step(nc.vector.tensor_reduce(st[:, 0, :], xs[:], AX.X, ALU.add))
                step(nc.vector.tensor_scalar(st[:, 1, :], st[:, 0, :], 1.0 / HID, None, ALU.mult))
                step(nc.vector.tensor_tensor(xc[:], xs[:], over(st[:, 1, :], HID), ALU.subtract))
                step(nc.vector.tensor_tensor(xq[:], xc[:], xc[:], ALU.mult))
                step(nc.vector.tensor_reduce(st[:, 2, :], xq[:], AX.X, ALU.add))
                step(nc.vector.tensor_scalar(st[:, 0, :], st[:, 2, :], 1.0 / HID, LN_EPS, ALU.mult, ALU.add))
                steps["var"] = count[0]
                dve.wait_ge(rstd_done, 1)
                step(nc.vector.tensor_tensor(xs[:], xc[:], over(st[:, 3, :], HID), ALU.mult))
                steps["xn"] = count[0]
                dve.wait_ge(const_in, 16)
                step(nc.vector.tensor_copy(negb[:], k("neg")))
                step(nc.vector.tensor_copy(identb[:], k("ident")))
                for q in range(1, 4, 2):
                    dve.wait_ge(xnT_ready, q + 1)
                    nc.vector.tensor_copy(xnT[:, q // 2, (q % 2) * 512:(q % 2) * 512 + 512], bank[q][:]).then_inc(xnT_used, 1)
                dve.wait_ge(ffn_in, NFFN)
                for kc in range(KC):
                    for mc in range(KC):
                        sign = (1.0 if not (kc and mc) else -1.0) / float(np.sqrt(HID))
                        nc.vector.tensor_scalar(hug[:, kc, mc, :], k("had"), su[:, kc:kc + 1], sign, ALU.mult, ALU.mult)\
                          .then_inc(hug_made, 1)
                c2 = coef[:].rearrange("p (i k) -> p k i", k=2)
                step(nc.vector.tensor_tensor(c2[:, 0, :], wsg, wsu, ALU.mult))
                step(nc.vector.scalar_tensor_tensor(out=c2[:, 1, :], in0=c2[:, 0, :], scalar=0.5, in1=sd, op0=ALU.mult, op1=ALU.mult))
                step(nc.vector.tensor_scalar(c2[:, 0, :], wsg, 0.5, None, ALU.mult))
                dve.wait_ge(ba_ready, 1)
                step(nc.vector.tensor_copy(ga[:, 0:2, :, :].rearrange("p k h u -> p u k h"),
                                           bank[4][:].rearrange("p (u k h) -> p u k h", u=UNITS, k=2)))
                steps["ba"] = count[0]
                gb = lambda a: a.unsqueeze(2).broadcast_to([P, PAIRS, UNITS])
                step(nc.vector.tensor_tensor(ga[:, 2, :, :], ga[:, 1, :, :], gb(ah[:, 1, :]), ALU.add))
                step(nc.vector.scalar_tensor_tensor(out=ga[:, 3, :, :], in0=ga[:, 2, :, :], scalar=-1.0, in1=ga[:, 2, :, :],
                                                    op0=ALU.mult, op1=ALU.max))
                steps["abs"] = count[0]
                step(nc.vector.tensor_scalar(ga[:, 2, :, :], ga[:, 2, :, :], 0.0, None, ALU.max))
                dve.wait_ge(a_step, 2)
                step(nc.vector.tensor_scalar(ga[:, 0, :, :], ga[:, 4, :, :], 1.0, None, ALU.add))
                step(nc.vector.reciprocal(scal[:, :, 1, :], ga[:, 0, :, :]))
                dve.wait_ge(a_step, 3)
                step(nc.vector.tensor_scalar(ga[:, 0, :, :], ga[:, 5, :, :], 2.0, None, ALU.add))
                step(nc.vector.reciprocal(ga[:, 6, :, :], ga[:, 0, :, :]))
                step(nc.vector.tensor_tensor(ga[:, 0, :, :], ga[:, 5, :, :], ga[:, 6, :, :], ALU.mult))
                step(nc.vector.tensor_tensor(ga[:, 1, :, :], ga[:, 0, :, :], ga[:, 0, :, :], ALU.mult))
                step(nc.vector.tensor_scalar(ga[:, 6, :, :], ga[:, 1, :, :], 1.0 / 17, 1.0 / 15, ALU.mult, ALU.add))
                for m in (13, 11, 9, 7, 5, 3, 1):
                    step(nc.vector.tensor_tensor(ga[:, 6, :, :], ga[:, 6, :, :], ga[:, 1, :, :], ALU.mult))
                    step(nc.vector.tensor_scalar(ga[:, 6, :, :], ga[:, 6, :, :], 1.0 / m, None, ALU.add))
                step(nc.vector.tensor_tensor(ga[:, 6, :, :], ga[:, 6, :, :], ga[:, 0, :, :], ALU.mult))
                step(nc.vector.scalar_tensor_tensor(out=ga[:, 6, :, :], in0=ga[:, 6, :, :], scalar=2.0, in1=ga[:, 2, :, :],
                                                    op0=ALU.mult, op1=ALU.add))
                step(nc.vector.tensor_scalar(ah[:, 2, :], ah[:, 0, :], -1.0, None, ALU.mult))
                step(nc.vector.tensor_tensor(ga[:, 7, :, :], ga[:, 6, :, :], gb(ah[:, 2, :]), ALU.mult))
                step(nc.vector.tensor_scalar(scal[:, :, 0, :], ga[:, 7, :, :], GATE_FLOOR, None, ALU.max))
                step(nc.vector.tensor_scalar(ga[:, 7, :, :], ga[:, 7, :, :], GATE_FLOOR, None, ALU.max))
                steps["g"] = count[0]
                dve.wait_ge(wd_used, 4)
                for h in (1, 2, 4):
                    src, dst = (wdT[:, 1], wdT[:, 0]) if h != 2 else (wdT[:, 0], wdT[:, 1])
                    s4 = src.rearrange("p (a t h) d -> p a t (h d)", t=2, h=h)
                    d4 = dst.rearrange("p (a t h) d -> p a t (h d)", t=2, h=h)
                    nc.vector.tensor_tensor(d4[:, :, 0], s4[:, :, 0], s4[:, :, 1], ALU.add)
                    step(nc.vector.tensor_tensor(d4[:, :, 1], s4[:, :, 0], s4[:, :, 1], ALU.subtract))
                nc.vector.scalar_tensor_tensor(
                    out=wdf[:].rearrange("p (i k) d -> p i (k d)", k=2), in0=wdT[:, 0], scalar=1.0 / float(np.sqrt(INTER)),
                    in1=wsd[:].unsqueeze(1).broadcast_to([P, IT, HID]), op0=ALU.mult, op1=ALU.mult).then_inc(wd_done, 1)
                dve.wait_ge(wd_done, 1)
                dve.wait_ge(res_in, 16)

            @block.gpsimd
            def _(pool):
                pool.wait_ge(const_in, 16)
                pool.wait_ge(v_step, steps["var"])
                nc.gpsimd.tensor_tensor(st[:, 3, :], st[:, 0, :], k("neghalf")[:, 0:TT], ALU.pow).then_inc(rstd_done, 1)

            @block.scalar
            def _(act):
                for q in range(0, 4, 2):
                    act.wait_ge(xnT_ready, q + 1)
                    nc.scalar.activation(xnT[:, q // 2, 0:512], bank[q][:], ACT.Copy).then_inc(xnT_used, 1)
                act.wait_ge(gate_in, 16 * 5)
                nc.scalar.activation(ah[:, 0, :], ah[:, 0, :], ACT.Exp).then_inc(a_step, 1)
                act.wait_ge(v_step, steps["ba"])
                nc.scalar.activation(ga[:, 4, :, :], ga[:, 0, :, :], ACT.Exp, scale=-1.0).then_inc(a_step, 1)
                act.wait_ge(v_step, steps["abs"])
                nc.scalar.activation(ga[:, 5, :, :], ga[:, 3, :, :], ACT.Exp, scale=-1.0).then_inc(a_step, 1)
                for m in range(KC * 2):
                    act.wait_ge(xh_ready, m + 1)
                    nc.scalar.activation(xh[:, m // 2, (m % 2) * 512:(m % 2) * 512 + 512], bank[m][:], ACT.Copy).then_inc(xh_done, 1)
                for m in range(4):
                    act.wait_ge(wd_ready, m + 1)
                    nc.scalar.activation(wdT[:, 1, 2 * m:2 * m + 2, :], bank[4 + m][:].rearrange("p (t d) -> p t d", t=2), ACT.Copy)\
                      .then_inc(wd_used, 1)
                act.wait_ge(cum_ready, 1)
                for m in range(2):
                    nc.scalar.activation(scal[:, :, 2 + m, :], bank[5][:, m * 256:m * 256 + 256].rearrange("p (h u) -> p h u", h=PAIRS),
                                         ACT.Exp).then_inc(a_step, 1)

            @block.tensor
            def _(pe):
                pe.wait_ge(const_in, 16)
                pe.wait_ge(v_step, steps["xn"])
                for q in range(4):
                    kc, t0 = q // 2, 4 * (q % 2)
                    for t in range(4):
                        last = nc.tensor.transpose(bank[q][:, t * P:t * P + P], xs[:, t0 + t, kc * P:kc * P + P], k("ident"))
                    last.then_inc(xnT_ready, 1)
                pe.wait_ge(xnT_used, 4)
                pe.wait_ge(gate_in, 16 * 5)
                for u in range(UNITS):
                    for h in range(2):
                        first = (u // NCH) * S + (u + h) % NCH * C
                        for kc in range(KC):
                            last = nc.tensor.matmul(bank[4][h * C:h * C + C, u * 2 * PAIRS:(u + 1) * 2 * PAIRS],
                                                    xnT[:, kc, first:first + C], wbas[:, kc, h, :], start=kc == 0, stop=kc == KC - 1)
                last.then_inc(ba_ready, 1)
                pe.wait_ge(hug_made, 4)
                for m in range(KC * 2):
                    for kc in range(KC):
                        last = nc.tensor.matmul(bank[m][:], hug[:, kc, m // 2, :], xnT[:, kc, (m % 2) * 512:(m % 2) * 512 + 512],
                                                start=kc == 0, stop=kc == KC - 1)
                    last.then_inc(xh_ready, 1)
                pe.wait_ge(v_step, steps["ba"])
                pe.wait_ge(ffn_in, NFFN)
                for m in range(4):
                    nc.tensor.matmul(bank[4 + m][:], k("had"), wdT[:, 0, 2 * m:2 * m + 2, :], start=True, stop=True).then_inc(wd_ready, 1)
                pe.wait_ge(wd_used, 4)
                pe.wait_ge(v_step, steps["g"])
                nc.tensor.matmul(bank[5][:, 0:256], k("cum_bd"), ga[:, 7, :, :], start=True, stop=True)
                nc.tensor.matmul(bank[5][:, 256:512], k("strict_bd"), ga[:, 7, :, :], start=True, stop=True).then_inc(cum_ready, 1)


def pairs(nc, sem, sb, bank, k, xnT, scal, negb, identb, yacc, xh, wdf, coef, wqkvz, conv, wout, nw, wgu):
    with ExitStack() as ctx:
        def tmp(name, shape, dt=F32):
            return sb(name, shape, dt, ctx)

        W4 = NCH * C
        SW = S + C
        NB = BASE
        cw = tmp("cw", [2, 3, 4])
        sc = tmp("sc", [2, 4, UNITS])
        woraw = tmp("woraw", [HID])
        wo = tmp("wo", [2, HID])
        zt = tmp("zt", [2, TT, P])
        AT = tmp("AT", [2, B, NCH, C])
        ME = tmp("ME", [2, B, NCH, C])
        X = tmp("X", [UNITS, NB])
        kg = tmp("kg", [2, B, NCH, C])
        LBo = tmp("LBo", [2, 2, UNITS, C])
        LBs = tmp("LBs", [2, 2, UNITS, C])
        R = tmp("R", [2, 2, UNITS, C])
        qs = tmp("qs", [2, TT, 2])
        hf = tmp("hf", [2, B, P])
        wfd = tmp("wfd", [2, HID // 2])
        wguT = tmp("wguT", [2, KC, P])
        fc = tmp("fc", [2])
        th = tmp("th", [B * P])
        wq = tmp("wq", [KC, 4, P])
        nwh = tmp("nwh", [1])
        kq = tmp("kq", [3, B, SW])
        ksqj = tmp("ksqj", [2, NCH, C])
        gm = tmp("gm", [2, NCH, C])
        gg = tmp("gg", [2, 2, NCH, C])
        gb_ = tmp("gb", [2, NCH, C])
        stat = tmp("stat", [6, UNITS])
        Xt = tmp("Xt", [2, NCH, C // NB + 1, NB])
        kc_ = tmp("kc", [2, NCH, C])
        XT = tmp("XT", [UNITS, NB])
        Tb = tmp("Tb", [UNITS, NB])
        prod = tmp("prod", [UNITS, NB])
        UT = tmp("UT", [B, 2, NCH, C])
        ET = tmp("ET", [2, NCH, C])
        EH = tmp("EH", [2, NCH, C // 2])
        LA = tmp("LA", [2, UNITS, C])
        sqo = tmp("sqo", [B * 2, D])
        ost = tmp("ost", [3, B * 2])
        og = tmp("og", [B, P])
        oTs = tmp("oTs", [2, B, P])

        names = """w_in cw_in sc_in wo_in nw_in wo_done proj_done tap0_done conv_step z_done wrap_done gm_done dg_done gexp_done
                   gram_done scale_step root_done gb_done at_done pt_done x_prod x_done me_done trk_done kc_done trv_done v_done
                   kg_done lb_done sqk_done sqq_done qst_done qs_done s0_zero tinit_done xt_ready xt_done sel_ready base_step t16_ready
                   tx_done u16_ready u16_done et_ready et_done up_ready up_done eh_ready eh_done lc_done hb_ready la_done w_ready
                   w_done dl_ready dl_done st_ready st_done o_ready osq_done ms_step ms_done rms_done on_done og_done ogT_ready
                   ogT_done op_ready acc_done nwh_done ff_in wfd_in ff_ready tanh_done gl_done hf_done turn pool_turn""".split()
        sems = {x: sem(x) for x in names}
        (w_in, cw_in, sc_in, wo_in, nw_in, wo_done, proj_done, tap0_done, conv_step, z_done, wrap_done, gm_done, dg_done, gexp_done,
         gram_done, scale_step, root_done, gb_done, at_done, pt_done, x_prod, x_done, me_done, trk_done, kc_done, trv_done, v_done,
         kg_done, lb_done, sqk_done, sqq_done, qst_done, qs_done, s0_zero, tinit_done, xt_ready, xt_done, sel_ready, base_step, t16_ready,
         tx_done, u16_ready, u16_done, et_ready, et_done, up_ready, up_done, eh_ready, eh_done, lc_done, hb_ready, la_done, w_ready,
         w_done, dl_ready, dl_done, st_ready, st_done, o_ready, osq_done, ms_step, ms_done, rms_done, on_done, og_done, ogT_ready,
         ogT_done, op_ready, acc_done, nwh_done, ff_in, wfd_in, ff_ready, tanh_done, gl_done, hf_done, turn, pool_turn) = (sems[x] for x in names)

        ring = [bank[0], bank[1]]
        DG, GR, TR = bank[2], bank[3], bank[4]
        XY, Z = [bank[5], bank[6]], bank[7]
        tok, dk = (slice(C, P), slice(0, C)), (slice(0, C), slice(C, P))
        H2 = C // 2
        top = tuple(slice(t.start, t.start + H2) for t in tok)
        low = tuple(slice(t.start + H2, t.start + C) for t in tok)

        NBLK = 2 * (P // NB)
        loads, free = [[]], 512
        for i in range(1, NB):
            if free < NBLK * (i + 1):
                loads.append([])
                free = 512
            loads[-1].append((i, 512 - free))
            free -= NBLK * (i + 1)
        NLOAD = len(loads)

        def slot(h, c):
            return (c - 1) % NCH if h == 0 else c

        def cols(h, w):
            a = (w + (h == 0)) * C
            return slice(a, a + C)

        def w4(ap, n=NCH):
            return ap.rearrange("p (u c) -> p u c", u=n)

        def over(a, n=C):
            return a.unsqueeze(2).broadcast_to([a.shape[0], a.shape[1], n])

        def each(a, n=NCH):
            return a.unsqueeze(1).broadcast_to([a.shape[0], n, a.shape[1]])

        def us(b):
            return slice(b * NCH, (b + 1) * NCH)

        body = """A.load A.proj.0 M.fload A.proj.1 A.proj.2 A.wrap.0 M.t16 M.u.0 A.gate.0 A.ksq.0 A.gram.0 M.u.1 A.at.0 A.val.0 A.proj.3
                  A.x.0 M.u.2 M.u.3 M.ea.0 M.ea.1 M.eb.0 A.gate.1 A.ksq.1 A.gram.1 A.at.1 M.ea.2 A.val.1 A.proj.4 A.x.1 M.eb.1 M.ea.3
                  A.proj.5 A.wrap.1 A.proj.6 M.eb.2 M.eb.3 M.ha.0 M.ha.1 M.hb.0 M.ha.2 M.hb.1 M.ha.3 M.hb.2 M.hb.3 M.w.0 A.gate.2 M.w.1
                  A.ksq.2 A.gram.2 M.w.2 A.at.2 M.w.3 M.delta.0 A.val.2 A.x.2 M.state.0 M.delta.1 A.gate.3 A.ksq.3 A.gram.3 M.state.1
                  M.norm.0 A.at.3 A.val.3 A.proj.7 M.delta.2 M.gated.0 A.ff A.x.3 M.state.2 M.turn.0 A.xt M.delta.3 A.sel.0 M.state.3
                  A.qsq M.norm.1 M.out.0 M.gated.1 A.sel.1 M.turn.1 A.sel.2 A.sel.3 A.sel.4 M.out.1""".split()
        assert NLOAD == 5

        def steps(do, kinds, n, q):
            for step in body:
                kind, name, *number = step.split(".")
                if kind in kinds and name in do:
                    do[name](*((n, q) if kind == "M" else (n + 1, 1 - q)), *map(int, number))

        def program(eng, do):
            steps(do, "A", -1, 1)
            with eng.Fori(0, PAIRS - 2, 2) as n:
                steps(do, "AM", n, 0)
                steps(do, "AM", n + 1, 1)
            steps(do, "AM", PAIRS - 2, 0)
            steps(do, "M", PAIRS - 1, 1)

        def wait(eng, sm, value):
            if not isinstance(value, int) or value > 0:
                eng.wait_ge(sm, value)

        with nc.Block() as block:
            @block.sync
            def _(sp):
                def some(m, n):
                    if isinstance(m, int):
                        return slice(m, m + n)
                    return bass.ds(nc.s_assert_within(m, 0, PAIRS - n, skip_runtime_bounds_check_because="the loop ends before it"), n)

                def load(m, q):
                    wait(sp, proj_done, m * 8)
                    sp.dma_start(wq[:], wqkvz[some(m, 1)].rearrange("o p c t m -> (o p) c t m")).then_inc(w_in, 16)
                    wait(sp, conv_step, m * 18)
                    sp.dma_start(cw[:, q], conv[some(m, 1)].rearrange("o p t m -> (o p) t m")).then_inc(cw_in, 16)
                    wait(sp, wo_done, m)
                    sp.dma_start(woraw[:], wout[some(m, 1)].rearrange("o p m -> (o p) m")).then_inc(wo_in, 16)
                    wait(sp, lb_done, m * 6 * B)
                    sp.dma_start(sc[:, q], scal[:, some(m, 1)].rearrange("p o k u -> p (o k) u")).then_inc(sc_in, 16)
                    if q == 0:
                        wait(sp, hf_done, m)
                        sp.dma_start(wguT[:], wgu[some(m, 2)].rearrange("j p c m -> p j c m")).then_inc(ff_in, 16)
                        sp.dma_start(fc[:], coef[:, some(m, 2)]).then_inc(ff_in, 16)

                def fload(n, q):
                    if q == 0:
                        sp.wait_ge(acc_done, n * 4 + 1)
                        sp.dma_start(wfd[:], wdf[:, some(n, 2)]).then_inc(wfd_in, 16)

                for h in range(2):
                    sp.dma_start(nwh[h * C:h * C + C, :], nw).then_inc(nw_in, 16)
                program(sp, {"load": load, "fload": fload})

            @block.tensor
            def _(pe):
                def alone():
                    pe.sem_inc(turn, 1)

                def proj(m, q, i):
                    if i == 0:
                        pe.wait_ge(w_in, (m + 1) * 16)
                        wait(pe, base_step, m * 2 * (NB - 1))
                    if i >= 2:
                        pe.wait_ge(conv_step, m * 18 + 3 * (i - 1))
                    dst = ring[i % 2]
                    if i < 6:
                        for kc in range(KC):
                            last = nc.tensor.matmul(dst[:], wq[:, kc, i % 3, :], xnT[:, kc, (i // 3) * 512:(i // 3) * 512 + 512],
                                                    start=kc == 0, stop=kc == KC - 1)
                    else:
                        for t in range(4):
                            tt = 4 * (i - 6) + t
                            for kc in range(KC):
                                last = nc.tensor.matmul(dst[:, t * P:t * P + P], xnT[:, kc, tt * P:tt * P + P], wq[:, kc, 3, :],
                                                        start=kc == 0, stop=kc == KC - 1)
                    last.then_inc(proj_done, 1)

                def ff(m, q):
                    if q == 0:
                        pe.wait_ge(ff_in, m * 16 + 32)
                    pe.wait_ge(z_done, (m + 1) * 2)
                    for j in range(2):
                        for kc in range(KC):
                            last = nc.tensor.matmul(ring[j][:], wguT[:, j, kc, :], xh[:, kc].rearrange("p (b t c) -> p b t c", b=B, t=2)[:, :, q, :],
                                                    start=kc == 0, stop=kc == KC - 1)
                    last.then_inc(ff_ready, 1)

                def turned(m, b, which, done):
                    for w in range(NCH):
                        last = nc.tensor.transpose(TR[:, w * P:w * P + P], kq[:, which, b, w * C:w * C + P], k("ident"))
                    last.then_inc(done, 1)

                def gate(m, q, b):
                    g = m * B + b
                    pe.wait_ge(gm_done, g + 1)
                    wait(pe, gexp_done, g)
                    nc.tensor.matmul(DG[:, 0:W4], k("strict_bd"), gm[:, b % 2], start=True, stop=False)
                    nc.tensor.matmul(DG[:, 0:W4], identb[:], each(negb[:]), start=False, stop=True)
                    nc.tensor.matmul(DG[:, W4:2 * W4], k("swap"), gm[:, b % 2], start=True, stop=True).then_inc(dg_done, 1)
                    pe.wait_ge(wrap_done, m * 2 + b // 2 + 1)
                    if b == 0:
                        wait(pe, qs_done, m)
                    else:
                        pe.wait_ge(v_done, 2 * g)
                    turned(m, b, 0, trk_done)

                def gram(m, q, b):
                    g = m * B + b
                    pe.wait_ge(wrap_done, m * 2 + b // 2 + 1)
                    wait(pe, pt_done, 2 * g)
                    alone()
                    for w in range(NCH):
                        for h in range(2):
                            last = nc.tensor.matmul(GR[tok[h], w * P:w * P + P], kq[dk[h], 0, b, cols(h, w)], kq[dk[h], 0:2, b, cols(h, w)],
                                                    start=True, stop=True)
                    last.then_inc(gram_done, 1)

                def val(m, q, b):
                    pe.wait_ge(kc_done, 2 * (m * B + b) + 2)
                    turned(m, b, 2, trv_done)

                def qsq(m, q):
                    pe.wait_ge(sqq_done, m + 1)
                    pe.wait_ge(xt_done, m + 1)
                    for t in range(TT):
                        last = nc.tensor.matmul(TR[:, 2 * t:2 * t + 2], kq[:, 1, t // 2, (t % 2) * P:(t % 2) * P + P], k("hsel"), start=True, stop=True)
                    last.then_inc(qst_done, 1)

                def xt(m, q):
                    pe.wait_ge(x_done, m * B + B)
                    pe.wait_ge(v_done, (m + 1) * 2 * B)
                    for z in range(2):
                        last = nc.tensor.transpose(TR[:, z * P:z * P + P], X[:, z * 8:z * 8 + 8, :].rearrange("p u c -> p (u c)"), k("ident"))
                    last.then_inc(xt_ready, 1)

                def sel(m, q, g):
                    if g == 0:
                        pe.wait_ge(xt_done, m + 1)
                        pe.wait_ge(hf_done, m + 1)
                    if g >= 2:
                        pe.wait_ge(base_step, m * 2 * (NB - 1) + 2 * loads[g - 2][-1][0] - 1)
                    for i, at in loads[g]:
                        last = nc.tensor.matmul(ring[g % 2][:, at:at + NBLK * (i + 1)], k("sel")[:, i * P:i * P + P], XT[:, :, 0:i + 1],
                                                start=True, stop=True)
                    last.then_inc(sel_ready, 1)

                def t16(n, q):
                    pe.wait_ge(base_step, (n + 1) * 2 * (NB - 1))
                    pe.wait_ge(on_done, n * 2 + 1)
                    for z in range(2):
                        last = nc.tensor.transpose(Z[:, z * P:z * P + P], Tb[:, z * 8:z * 8 + 8, :].rearrange("p u c -> p (u c)"), k("ident"))
                    last.then_inc(t16_ready, 1)

                def u(n, q, b):
                    pe.wait_ge(tx_done, n * B + b + 1)
                    if b >= 2:
                        pe.wait_ge(u16_done, n * B + b - 1)
                    elif b == 0:
                        pe.wait_ge(acc_done, n * 4 + 1)
                    alone()
                    for w in range(NCH):
                        for h in range(2):
                            last = nc.tensor.matmul(XY[b % 2][tok[h], w * C:w * C + C], UT[tok[h], b, 1, w, :], k("eye")[tok[h]], start=True, stop=True)
                    last.then_inc(u16_ready, 1)

                def ea(n, q, b):
                    pe.wait_ge(me_done, n * B + b + 1)
                    if b:
                        pe.wait_ge(et_done, n * B + b)
                    else:
                        pe.wait_ge(tx_done, n * B + B)
                    alone()
                    for w in range(NCH):
                        for h in range(2):
                            last = nc.tensor.matmul(Z[tok[h], w * C:w * C + C], ME[tok[h], q, b, w, :], UT[tok[h], b, 1, w, :], start=True, stop=True)
                    last.then_inc(et_ready, 1)

                def eb(n, q, b):
                    pe.wait_ge(et_done, n * B + b + 1)
                    if b < 2:
                        pe.wait_ge(u16_done, n * B + b + 3)
                    else:
                        pe.wait_ge(up_done, n * B + b - 1)
                    alone()
                    for w in range(NCH):
                        for h in range(2):
                            nc.tensor.matmul(XY[b % 2][tok[h], w * C:w * C + C], ET[tok[h], b % 2, w, :], UT[tok[h], b, 0, w, :], start=True, stop=True)
                            last = nc.tensor.matmul(XY[b % 2][tok[h], W4 + w * C:W4 + w * C + C], UT[tok[h], b, 0, w, :], ET[tok[h], b % 2, w, :],
                                                    start=True, stop=True)
                    last.then_inc(up_ready, 1)

                def ha(n, q, b):
                    pe.wait_ge(up_done, n * B + b + 1)
                    if b:
                        pe.wait_ge(eh_done, n * B + b)
                    else:
                        pe.wait_ge(et_done, n * B + B)
                    alone()
                    for w in range(NCH):
                        for h in range(2):
                            last = nc.tensor.matmul(Z[low[h], w * H2:w * H2 + H2], AT[top[h], q, b, w, H2:C], UT[top[h], b, 1, w, 0:H2], start=True, stop=True)
                    last.then_inc(eh_ready, 1)

                def hb(n, q, b):
                    pe.wait_ge(eh_done, n * B + b + 1)
                    if b < 2:
                        pe.wait_ge(up_done, n * B + b + 3)
                    else:
                        pe.wait_ge(la_done, 2 * (n * B + b - 1))
                    alone()
                    for w in range(NCH):
                        for h in range(2):
                            last = nc.tensor.matmul(XY[b % 2][top[h], w * H2:w * H2 + H2], EH[low[h], b % 2, w, :], UT[low[h], b, 0, w, H2:C],
                                                    start=True, stop=True)
                    last.then_inc(hb_ready, 1)

                def w(n, q, b):
                    pe.wait_ge(la_done, 2 * (n * B + b) + 2)
                    pe.wait_ge(kg_done, n * B + b + 1)
                    if b:
                        pe.wait_ge(w_done, 2 * (n * B + b))
                    else:
                        pe.wait_ge(eh_done, n * B + B)
                    alone()
                    for v in range(NCH):
                        for h in range(2):
                            last = nc.tensor.matmul(Z[dk[h], v * C:v * C + C], kg[tok[h], q, b, v, :], LA[tok[h], h, b * NCH + v, :], start=True, stop=True)
                    last.then_inc(w_ready, 1)

                def delta(n, q, c):
                    if c == 0:
                        pe.wait_ge(w_done, 2 * (n * B + B))
                        pe.wait_ge(la_done, 2 * (n * B + B))
                    else:
                        pe.wait_ge(st_done, 2 * (n * (NCH - 1) + c))
                    if c == 3:
                        pe.wait_ge(ogT_done, n * 2 + 1)
                    for b in range(B):
                        for h in range(2):
                            v = b * NCH + slot(h, c)
                            last = nc.tensor.matmul(XY[0][tok[h], b * C:b * C + C], LA[:, h, v, :], R[:, q, h, v, :], start=True, stop=True)
                    last.then_inc(dl_ready, 1)

                def state(n, q, c):
                    pe.wait_ge(dl_done, 2 * (n * NCH + c) + 2)
                    if c == 0:
                        pe.wait_ge(lb_done, (n + 1) * 6 * B)
                    if c < NCH - 1:
                        for b in range(B):
                            for h in range(2):
                                v = b * NCH + slot(h, c)
                                last = nc.tensor.matmul(XY[1][dk[h], b * C:b * C + C], LBs[:, q, h, v, :], R[:, q, h, v, :], start=True, stop=True)
                        last.then_inc(st_ready, 1)
                    if c == 2:
                        pe.wait_ge(on_done, n * 2 + 2)
                    for b in range(B):
                        for h in range(2):
                            v = b * NCH + slot(h, c)
                            r = (c % 2) * C
                            last = nc.tensor.matmul(Z[r:r + C, b * P + h * C:b * P + h * C + C], LBo[:, q, h, v, :], R[:, q, h, v, :],
                                                    start=True, stop=True)
                    last.then_inc(o_ready, 1)

                def turn_(n, q, t):
                    pe.wait_ge(og_done, n * 2 + t + 1)
                    if t:
                        pe.wait_ge(acc_done, n * 4 + 3)
                    else:
                        pe.wait_ge(dl_done, 2 * (n * NCH + 3))
                    for b in range(B):
                        last = nc.tensor.transpose(XY[0][:, b * P:b * P + P], og[:, b, :], k("ident"))
                    last.then_inc(ogT_ready, 1)

                def out(n, q, t):
                    pe.wait_ge(ogT_done, n * 2 + t + 1)
                    pe.wait_ge(wo_done, n + 1)
                    if t:
                        pe.wait_ge(acc_done, n * 4 + 2)
                    else:
                        pe.wait_ge(dl_done, 2 * (n * NCH + NCH))
                    if t == q:
                        pe.wait_ge(hf_done, n + 1)
                        if q == 0:
                            pe.wait_ge(wfd_in, n * 8 + 16)
                    for j in range(2):
                        for b in range(2 * j, 2 * j + 2):
                            dst = XY[1 - j][:, (b % 2) * HID:(b % 2) * HID + HID]
                            last = nc.tensor.matmul(dst, oTs[:, t, b, :], wo[:, q, :], start=True, stop=t != q)
                            if t == q:
                                last = nc.tensor.matmul(dst, hf[:, q, b, :], wfd[:].rearrange("p k d -> p (k d)"), start=False, stop=True)
                        last.then_inc(op_ready, 1)

                pe.wait_ge(s0_zero, 1)
                program(pe, {"proj": proj, "ff": ff, "gate": gate, "gram": gram, "val": val, "qsq": qsq, "xt": xt, "sel": sel, "t16": t16, "u": u,
                             "ea": ea, "eb": eb, "ha": ha, "hb": hb, "w": w, "delta": delta, "state": state, "turn": turn_, "out": out})

            @block.scalar
            def _(act):
                def proj(m, q, i):
                    act.wait_ge(proj_done, m * 8 + i + 1)
                    if i < 6:
                        if i == 0:
                            act.wait_ge(cw_in, (m + 1) * 16)
                            wait(act, gram_done, m * B)
                            wait(act, trv_done, m * B)
                            wait(act, qst_done, m)
                            wait(act, lb_done, m * 6 * B)
                        nc.scalar.activation(kq[:, i % 3, 2 * (i // 3):2 * (i // 3) + 2, 0:S], w4(ring[i % 2][:], 2), ACT.Copy,
                                             scale=cw[:, q, i % 3, 3:4]).then_inc(tap0_done, 1)
                    else:
                        nc.scalar.activation(zt[:, q, 4 * (i - 6):4 * (i - 6) + 4, :], w4(ring[i % 2][:], 4), ACT.Tanh, scale=0.5).then_inc(z_done, 1)
                    if i == 7:
                        act.wait_ge(wo_in, (m + 1) * 16)
                        nc.scalar.activation(wo[:, q], woraw[:], ACT.Copy, scale=nwh[:]).then_inc(wo_done, 1)

                def ff(m, q):
                    act.wait_ge(ff_ready, m + 1)
                    wait(act, hf_done, m)
                    nc.scalar.activation(th[:], ring[0][:], ACT.Tanh, scale=fc[:, 0:1]).then_inc(tanh_done, 1)

                def gate(m, q, b):
                    g = m * B + b
                    act.wait_ge(dg_done, g + 1)
                    wait(act, lb_done, 6 * (g - 1))
                    nc.scalar.activation(gg[:, b % 2], DG[:].rearrange("p (k u c) -> p k u c", k=2, u=NCH), ACT.Exp).then_inc(gexp_done, 1)
                    act.wait_ge(trk_done, g + 1)
                    for h in range(2):
                        nc.scalar.activation(kc_[tok[h], b % 2], w4(TR[:])[tok[h], :, h * C:h * C + C], ACT.Copy).then_inc(kc_done, 1)

                def ksq(m, q, b):
                    g = m * B + b
                    act.wait_ge(kc_done, 2 * g + 2)
                    wait(act, scale_step, 4 * (g - 3) - 3)
                    wait(act, sqk_done, 4 * (g - 1))
                    for w in range(NCH):
                        nc.scalar.activation(ksqj[:, b % 2, w], kc_[:, b % 2, w], ACT.Square, accum_out=stat[:, 0, b * NCH + w:b * NCH + w + 1]).then_inc(sqk_done, 1)

                def qsq(m, q):
                    act.wait_ge(lb_done, (m + 1) * 6 * B)
                    act.wait_ge(gram_done, (m + 1) * B)
                    nc.scalar.activation(kq[:, 1, :, 0:S], kq[:, 1, :, 0:S], ACT.Square).then_inc(sqq_done, 1)

                def xt(m, q):
                    act.wait_ge(xt_ready, m + 1)
                    nc.scalar.activation(XT[:], w4(TR[:, 0:UNITS * NB], UNITS), ACT.Copy).then_inc(xt_done, 1)

                def u(n, q, b):
                    act.wait_ge(u16_ready, n * B + b + 1)
                    nc.scalar.activation(UT[:, b, 0], w4(XY[b % 2][:, 0:W4]), ACT.Copy).then_inc(u16_done, 1)

                def ea(n, q, b):
                    act.wait_ge(et_ready, n * B + b + 1)
                    if b >= 2:
                        act.wait_ge(up_ready, n * B + b - 1)
                    nc.scalar.activation(ET[:, b % 2], w4(Z[:, 0:W4]), ACT.Copy).then_inc(et_done, 1)

                def ha(n, q, b):
                    act.wait_ge(up_done, n * B + b + 1)
                    for h in range(2):
                        nc.scalar.activation(LA[tok[h], h, us(b), :], UT[tok[h], b, 0], ACT.Copy).then_inc(lc_done, 1)
                    act.wait_ge(eh_ready, n * B + b + 1)
                    if b >= 2:
                        act.wait_ge(hb_ready, n * B + b - 1)
                    nc.scalar.activation(EH[:, b % 2], w4(Z[:, 0:NCH * H2]), ACT.Copy).then_inc(eh_done, 1)

                def w(n, q, b):
                    act.wait_ge(w_ready, n * B + b + 1)
                    for h in range(2):
                        nc.scalar.activation(LA[dk[h], h, us(b), :], w4(Z[dk[h], 0:W4]), ACT.Copy, scale=-1.0).then_inc(w_done, 1)

                def delta(n, q, c):
                    act.wait_ge(dl_ready, n * NCH + c + 1)
                    dst = R[tok[0], q, 0].rearrange("p (b c) d -> p b c d", b=B)[:, :, slot(0, c), :]
                    nc.scalar.activation(dst, w4(XY[0][tok[0], 0:W4]), ACT.Copy).then_inc(dl_done, 1)

                def state(n, q, c):
                    if c < NCH - 1:
                        act.wait_ge(st_ready, n * (NCH - 1) + c + 1)
                        dst = R[dk[0], q, 0].rearrange("p (b c) d -> p b c d", b=B)[:, :, slot(0, c + 1), :]
                        nc.scalar.activation(dst, w4(XY[1][dk[0], 0:W4]), ACT.Copy).then_inc(st_done, 1)

                def norm(n, q, t):
                    act.wait_ge(o_ready, n * NCH + 2 * t + 2)
                    if t:
                        act.wait_ge(ms_step, n * 2 + 1)
                    nc.scalar.activation(sqo[:], Z[:].rearrange("p (b d) -> p b d", d=D), ACT.Square).then_inc(osq_done, 1)

                def turn_(n, q, t):
                    act.wait_ge(ogT_ready, n * 2 + t + 1)
                    nc.scalar.activation(oTs[:, t], w4(XY[0][:], B), ACT.Copy).then_inc(ogT_done, 1)

                act.wait_ge(nw_in, 32)
                nc.scalar.activation(nwh[:], nwh[:], ACT.Copy, scale=0.5).then_inc(nwh_done, 1)
                act.wait_ge(nwh_done, 1)
                program(act, {"proj": proj, "ff": ff, "gate": gate, "ksq": ksq, "qsq": qsq, "xt": xt, "u": u, "ea": ea, "ha": ha, "w": w,
                              "delta": delta, "state": state, "norm": norm, "turn": turn_})

            @block.gpsimd
            def _(pool):
                def alone():
                    pool.sem_inc(pool_turn, 1)

                def wrap(m, q, j):
                    pool.wait_ge(conv_step, m * 18 + 9 * (j + 1))
                    rows = slice(2 * j, 2 * j + 2)
                    alone()
                    nc.gpsimd.tensor_copy(kq[:, :, rows, S:SW], kq[:, :, rows, 0:C]).then_inc(wrap_done, 1)

                def gate(m, q, b):
                    g = m * B + b
                    if b == 0:
                        pool.wait_ge(sc_in, (m + 1) * 16)
                    wait(pool, dg_done, g - 1)
                    nc.gpsimd.tensor_tensor(gm[:, b % 2], over(sc[:, q, 0, us(b)]), each(k("cum")), ALU.mult).then_inc(gm_done, 1)

                def ksq(m, q, b):
                    g = m * B + b
                    pool.wait_ge(scale_step, 4 * g + 1)
                    wait(pool, v_done, 2 * (g - 3))
                    nc.gpsimd.tensor_tensor(stat[:, 2, us(b)], stat[:, 5, us(b)], k("half")[:, us(b)], ALU.pow).then_inc(root_done, 1)

                def gram(m, q, b):
                    g = m * B + b
                    pool.wait_ge(gexp_done, g + 1)
                    pool.wait_ge(scale_step, 4 * g + 3)
                    wait(pool, pt_done, 2 * (g - 1))
                    nc.gpsimd.tensor_tensor(gb_[:, b % 2], gg[:, b % 2, 0], over(stat[:, 3, us(b)]), ALU.mult).then_inc(gb_done, 1)
                    pool.wait_ge(kc_done, 2 * g + 2)
                    nc.gpsimd.tensor_tensor(kg[:, q, b], kc_[:, b % 2], over(sc[:, q, 2, us(b)]), ALU.mult).then_inc(kg_done, 1)

                def val(m, q, b):
                    g = m * B + b
                    pool.wait_ge(at_done, g + 1)
                    wait(pool, x_done, g - 1)
                    nc.gpsimd.tensor_tensor(Xt[:, b % 2, :, 0:C // NB, :], AT[:, q, b].rearrange("p u (k c) -> p u k c", c=NB),
                                            each(k("base")).rearrange("p u (k c) -> p u k c", c=NB), ALU.mult).then_inc(x_prod, 1)
                    nc.gpsimd.tensor_tensor(ME[:, q, b], AT[:, q, b], each(k("merge")), ALU.mult).then_inc(me_done, 1)
                    pool.wait_ge(me_done, g + 1)
                    pool.wait_ge(scale_step, 4 * g + 4)
                    for half in range(2):
                        hq, hk = (0, 1) if half == 0 else (1, 0)
                        if half:
                            pool.wait_ge(lb_done, 6 * g + 3)
                        nc.gpsimd.tensor_tensor(LBo[dk[hq], q, hq, us(b), :], w4(kq[dk[hq], 1, b, (1 - hq) * C:(1 - hq) * C + S]),
                                                gg[dk[hq], b % 2, 1], ALU.mult).then_inc(lb_done, 1)
                        nc.gpsimd.tensor_tensor(LBs[dk[hq], q, hq, us(b), :], each(k("eye")[dk[hq]]),
                                                gg[dk[hq], b % 2, 1, :, C - 1:C].broadcast_to([C, NCH, C]), ALU.mult).then_inc(lb_done, 1)
                        nc.gpsimd.tensor_tensor(LBs[tok[hk], q, hk, us(b), :], kc_[tok[hk], b % 2], over(stat[tok[hk], 4, us(b)]), ALU.mult)\
                          .then_inc(lb_done, 1)
                    pool.wait_ge(lb_done, 6 * g + 6)

                def xt(m, q):
                    wait(pool, t16_ready, m)
                    alone()
                    nc.gpsimd.tensor_copy(Tb[:], each(k("tinit"), UNITS)).then_inc(tinit_done, 1)

                def norm(n, q, t):
                    pool.wait_ge(ms_done, n * 2 + t + 1)
                    nc.gpsimd.tensor_tensor(ost[:, 2, :], ost[:, 1, :], k("neghalf")[:, 0:B * 2], ALU.pow).then_inc(rms_done, 1)

                nc.gpsimd.memset(R[:], 0.0).then_inc(s0_zero, 1)
                for j in range(2):
                    nc.gpsimd.tensor_copy(Xt[:, j, :, C // NB, :], each(k("diag"))).then_inc(s0_zero, 1)
                program(pool, {"wrap": wrap, "ksq": ksq, "gate": gate, "gram": gram, "val": val, "xt": xt, "norm": norm})

            @block.vector
            def _(dve):
                def proj(m, q, i):
                    if i >= 6:
                        return
                    y = kq[:, i % 3, 2 * (i // 3):2 * (i // 3) + 2, :]
                    p = w4(ring[i % 2][:], 2)
                    dve.wait_ge(tap0_done, m * 6 + i + 1)
                    for t in (1, 2, 3):
                        nc.vector.scalar_tensor_tensor(out=y[:, :, t:S], in0=p[:, :, 0:S - t], scalar=cw[:, q, i % 3, 3 - t:4 - t],
                                                       in1=y[:, :, t:S], op0=ALU.mult, op1=ALU.add).then_inc(conv_step, 1)
                        dve.wait_ge(conv_step, m * 18 + 3 * i + t)

                def ff(m, q):
                    dve.wait_ge(tanh_done, m + 1)
                    nc.vector.scalar_tensor_tensor(out=th[:], in0=th[:], scalar=1.0, in1=ring[0][:], op0=ALU.add, op1=ALU.mult).then_inc(gl_done, 1)
                    dve.wait_ge(gl_done, m + 1)
                    nc.vector.scalar_tensor_tensor(out=hf[:, q], in0=w4(ring[1][:], B), scalar=fc[:, 1:2], in1=w4(th[:], B),
                                                   op0=ALU.mult, op1=ALU.mult).then_inc(hf_done, 1)

                def ksq(m, q, b):
                    g = m * B + b
                    base = 4 * g
                    dve.wait_ge(sqk_done, 4 * g + 4)
                    wait(dve, lb_done, 6 * (g - 3))
                    nc.vector.tensor_scalar(stat[:, 5, us(b)], stat[:, 0, us(b)], EPS, None, ALU.add).then_inc(scale_step, 1)
                    dve.wait_ge(scale_step, base + 1)
                    nc.vector.reciprocal(stat[:, 1, us(b)], stat[:, 5, us(b)]).then_inc(scale_step, 1)
                    dve.wait_ge(scale_step, base + 2)
                    if b == 0:
                        dve.wait_ge(sc_in, (m + 1) * 16)
                    nc.vector.tensor_tensor(stat[:, 3, us(b)], stat[:, 1, us(b)], sc[:, q, 1, us(b)], ALU.mult).then_inc(scale_step, 1)
                    dve.wait_ge(scale_step, base + 3)
                    nc.vector.tensor_tensor(stat[:, 4, us(b)], stat[:, 3, us(b)], sc[:, q, 3, us(b)], ALU.mult).then_inc(scale_step, 1)

                def qsq(m, q):
                    dve.wait_ge(qst_done, m + 1)
                    nc.vector.tensor_scalar(qs[:, q], TR[:, 0:2 * TT].rearrange("p (t h) -> p t h", h=2), EPS, EPS * D, ALU.add, ALU.mult).then_inc(qs_done, 1)

                def at(m, q, b):
                    g = m * B + b
                    gr = GR[:].rearrange("p (u k c) -> p u k c", u=NCH, k=2)
                    dve.wait_ge(gram_done, g + 1)
                    dve.wait_ge(gb_done, g + 1)
                    nc.vector.tensor_tensor(AT[:, q, b], gr[:, :, 0, :], gb_[:, b % 2], ALU.mult).then_inc(at_done, 1)
                    for h in range(2):
                        nc.vector.tensor_tensor(LBo[tok[h], q, h, us(b), :], gr[tok[h], :, 1, :], gb_[tok[h], b % 2], ALU.mult).then_inc(pt_done, 1)

                def val(m, q, b):
                    g = m * B + b
                    dve.wait_ge(trv_done, g + 1)
                    dve.wait_ge(root_done, g + 1)
                    for h in range(2):
                        nc.vector.tensor_tensor(R[tok[h], q, h, us(b), :], w4(TR[:])[tok[h], :, h * C:h * C + C], over(stat[tok[h], 2, us(b)]),
                                                ALU.mult).then_inc(v_done, 1)

                def x(m, q, b):
                    dve.wait_ge(x_prod, m * B + b + 1)
                    if b == 0:
                        wait(dve, xt_ready, m)
                    nc.vector.tensor_reduce(X[:, us(b), :], Xt[:, b % 2].rearrange("p u k c -> p u c k"), AX.X, ALU.add).then_inc(x_done, 1)

                def sel(m, q, g):
                    if g == 0:
                        dve.wait_ge(tinit_done, m + 1)
                    dve.wait_ge(sel_ready, m * NLOAD + g + 1)
                    for i, at in loads[g]:
                        base = m * 2 * (NB - 1) + 2 * (i - 1)
                        if i > 1:
                            dve.wait_ge(base_step, base)
                        nc.vector.tensor_tensor(prod[:, :, 0:i + 1], w4(ring[g % 2][:, at:at + NBLK * (i + 1)], NBLK), Tb[:, :, 0:i + 1], ALU.mult)\
                          .then_inc(base_step, 1)
                        dve.wait_ge(base_step, base + 1)
                        nc.vector.tensor_reduce(Tb[:, :, i], prod[:, :, 0:i + 1], AX.X, ALU.add, negate=True).then_inc(base_step, 1)

                def t16(n, q):
                    dve.wait_ge(t16_ready, n + 1)
                    for b in range(B):
                        src = w4(Z[:, b * NCH * NB:(b + 1) * NCH * NB]).unsqueeze(2).broadcast_to([P, NCH, C // NB, NB])
                        nc.vector.tensor_tensor(UT[:, b, 1].rearrange("p u (k c) -> p u k c", c=NB), src,
                                                each(k("base_d")).rearrange("p u (k c) -> p u k c", c=NB), ALU.mult).then_inc(tx_done, 1)

                def eb(n, q, b):
                    dve.wait_ge(up_ready, n * B + b + 1)
                    nc.vector.tensor_tensor(UT[:, b], UT[:, b], XY[b % 2][:].rearrange("p (k u c) -> p k u c", k=2, u=NCH), ALU.subtract).then_inc(up_done, 1)

                def hb(n, q, b):
                    dve.wait_ge(hb_ready, n * B + b + 1)
                    dve.wait_ge(lc_done, 2 * (n * B + b) + 2)
                    for h in range(2):
                        nc.vector.tensor_scalar(LA[top[h], h, us(b), H2:C], w4(XY[b % 2][top[h], 0:NCH * H2]), -1.0, None, ALU.mult).then_inc(la_done, 1)

                def delta(n, q, c):
                    dve.wait_ge(dl_ready, n * NCH + c + 1)
                    dst = R[tok[1], q, 1].rearrange("p (b c) d -> p b c d", b=B)[:, :, slot(1, c), :]
                    nc.vector.tensor_copy(dst, w4(XY[0][tok[1], 0:W4])).then_inc(dl_done, 1)

                def state(n, q, c):
                    if c < NCH - 1:
                        dve.wait_ge(st_ready, n * (NCH - 1) + c + 1)
                        dst = R[dk[1], q, 1].rearrange("p (b c) d -> p b c d", b=B)[:, :, slot(1, c + 1), :]
                        nc.vector.tensor_copy(dst, w4(XY[1][dk[1], 0:W4])).then_inc(st_done, 1)

                def norm(n, q, t):
                    dve.wait_ge(osq_done, n * 2 + t + 1)
                    nc.vector.tensor_reduce(ost[:, 0, :], sqo[:], AX.X, ALU.add).then_inc(ms_step, 1)
                    dve.wait_ge(ms_step, n * 2 + t + 1)
                    h2 = lambda a: a.rearrange("p (b h) -> p b h", h=2)
                    nc.vector.scalar_tensor_tensor(out=h2(ost[:, 1, :]), in0=h2(ost[:, 0, :]), scalar=1.0 / D,
                                                   in1=qs[:, q].rearrange("p (b t) h -> p b t h", t=2)[:, :, t, :], op0=ALU.mult, op1=ALU.add).then_inc(ms_done, 1)

                def gated(n, q, t):
                    dve.wait_ge(rms_done, n * 2 + t + 1)
                    if t:
                        dve.wait_ge(ogT_ready, n * 2 + 1)
                    o = og[:].rearrange("p b (h d) -> p (b h) d", h=2)
                    nc.vector.tensor_tensor(o, Z[:].rearrange("p (b d) -> p b d", d=D), over(ost[:, 2, :]), ALU.mult).then_inc(on_done, 1)
                    dve.wait_ge(on_done, n * 2 + t + 2)
                    nc.vector.scalar_tensor_tensor(out=og[:], in0=zt[:, q].rearrange("p (b t) m -> p b t m", t=2)[:, :, t, :], scalar=1.0, in1=og[:],
                                                   op0=ALU.add, op1=ALU.mult).then_inc(og_done, 1)

                def out(n, q, t):
                    for j in range(2):
                        dve.wait_ge(op_ready, n * 4 + 2 * t + j + 1)
                        y = yacc[:].rearrange("p (b t) m -> p b t m", t=2)[:, 2 * j:2 * j + 2, t, :]
                        nc.vector.tensor_tensor(y, y, w4(XY[1 - j][:], 2), ALU.add).then_inc(acc_done, 1)

                dve.wait_ge(s0_zero, 3)
                dve.sem_inc(on_done, 1)
                dve.sem_inc(acc_done, 1)
                program(dve, {"proj": proj, "ff": ff, "ksq": ksq, "qsq": qsq, "at": at, "val": val, "x": x, "sel": sel, "t16": t16, "eb": eb, "hb": hb,
                              "delta": delta, "state": state, "norm": norm, "gated": gated, "out": out})


def finish(nc, sem, yacc, out):
    out_done = sem("out_done")
    with nc.Block() as block:
        @block.sync
        def _(sp):
            sp.dma_start(out.rearrange("(t p) d -> p t d", p=P), yacc[:]).then_inc(out_done, 16)
            sp.wait_ge(out_done, 16)


def kernel(L0_attn_hidden_states, L0_attn_w_qkvz, L0_attn_w_ba, L0_attn_conv_w, L0_attn_A_log, L0_attn_dt_bias,
           L0_attn_norm_weight, L0_attn_w_out, L0_ffn_SU_ug, L0_ffn_SU_dp, L0_ffn_Wscale_ug, L0_ffn_Wscale_dp,
           L0_ffn_W_up, L0_ffn_W_gate, L0_ffn_W_down):
    import concourse.bacc as bacc
    from concourse.bass_utils import run_bass_kernel_spmd

    def lay(a):
        return np.ascontiguousarray(a)

    a = np.asarray
    w = a(L0_attn_w_qkvz).reshape(PAIRS, 2, 4, D, KC, P)[:, :, [1, 0, 2, 3]].transpose(0, 5, 4, 2, 1, 3).reshape(PAIRS, P, KC, 4, P)
    ba = a(L0_attn_w_ba).reshape(PAIRS, 2, 2, KC, P)[:, ::-1].transpose(4, 3, 1, 2, 0).reshape(P, KC, 2, 2 * PAIRS)
    cv = a(L0_attn_conv_w).reshape(3, PAIRS, P, 4)[[1, 0, 2]].transpose(1, 2, 0, 3)
    arrays = {
        "x": lay(a(L0_attn_hidden_states).reshape(NTOK, HID)),
        "wqkvz": lay(w), "wba": lay(ba), "conv": lay(cv),
        "alog": lay(a(L0_attn_A_log).reshape(PAIRS, 2).T), "dtb": lay(a(L0_attn_dt_bias).reshape(PAIRS, 2).T),
        "nw": lay(a(L0_attn_norm_weight).reshape(D, 1)),
        "wout": lay(a(L0_attn_w_out).reshape(HID, PAIRS, P).transpose(1, 2, 0)),
        "su_ug": lay(a(L0_ffn_SU_ug).reshape(KC, P).T), "su_dp": lay(a(L0_ffn_SU_dp).reshape(IT, P).T),
        "ws_up": lay(a(L0_ffn_Wscale_ug)[:INTER].reshape(IT, P).T), "ws_gate": lay(a(L0_ffn_Wscale_ug)[INTER:].reshape(IT, P).T),
        "ws_dp": lay(a(L0_ffn_Wscale_dp).reshape(1, HID)),
        "wgu": lay(np.stack([a(L0_ffn_W_gate), a(L0_ffn_W_up)]).reshape(2, IT, P, KC, P).transpose(1, 0, 4, 3, 2).reshape(2 * IT, P, KC, P)),
        "wdown": lay(a(L0_ffn_W_down).reshape(HID, IT, P).transpose(2, 1, 0)),
        "consts": constants(),
    }
    nc = bacc.Bacc("TRN2", target_bir_lowering=False, num_devices=1)
    args = [nc.dram_tensor(f"{n}_dram", v.shape, mybir.dt.from_np(v.dtype), kind="ExternalInput").ap() for n, v in arrays.items()]
    out = nc.dram_tensor("out_dram", (NTOK, HID), F32, kind="ExternalOutput").ap()
    build(nc, *args, out)
    r = run_bass_kernel_spmd(nc, [{f"{n}_dram": v for n, v in arrays.items()}], core_ids=[0])
    return r.results[0]["out_dram"].reshape(B, S, HID)
```
